# Optimizing a Trainium2 kernel written in Bass

```python
import numpy as np
import jax
import jax.numpy as jnp

def _softmax(x, axis=-1):
    return jax.nn.softmax(x, axis=axis)

def _gelu(x):
    return jax.nn.gelu(x, approximate=True)

def _silu(x):
    return jax.nn.silu(x)

def _sigmoid(x):
    return jax.nn.sigmoid(x)

def _layernorm(x, axis=-1, eps=1e-05):
    m = jnp.mean(x, axis=axis, keepdims=True)
    v = jnp.var(x, axis=axis, keepdims=True)
    return (x - m) / jnp.sqrt(v + eps)

def _scatter_add(tgt, idx, src, axis=0):
    return tgt.at[idx].add(src)

def _segment_sum(src, seg, n):
    return jax.ops.segment_sum(src, seg, n)
kernel_name = 'mk_adj_ffn_d1_adj_r2_70d53b'

def setup_inputs(seed: int=0):
    np.random.seed(seed)
    _w = jnp.asarray

    def _rec_inputs():
        import jax
        import jax.numpy as jnp
        _gk = jax.random.key(seed)
        x = 7.22e-05 + 1 * jax.random.normal(jax.random.fold_in(_gk, 1), (16, 512, 128), jnp.float32)
        _w = (1.0 + jnp.arange(512, dtype=jnp.float32)) ** (-0.5)
        _w = _w / _w.mean()
        _pij = jnp.clip(0.015625 * _w[:, None] * _w[None, :], 0.0, 1.0)
        _a = jax.random.uniform(jax.random.fold_in(_gk, 2), (16, 512, 512)) < _pij
        _a = jnp.logical_or(_a, jnp.swapaxes(_a, -1, -2))
        _a = jnp.logical_or(_a, jnp.eye(512, dtype=bool))
        _af = _a.astype(jnp.float32)
        adj = _af
        return (x, adj)
    x, adj = _rec_inputs()

    def _L0_gnn_setup():
        import jax, jax.numpy as jnp
        import numpy as np
        from jax import lax
        DIM = 128
        EPS = 1e-05

        def _bn(h, g, b, m, v):
            scale = g / jnp.sqrt(v + EPS)
            return h * scale[None, :, None] + (b - m * scale)[None, :, None]

        def _conv1d(h, w, pad):
            return lax.conv_general_dilated(h, w, window_strides=(1,), padding=[(pad, pad)], dimension_numbers=('NCH', 'OIH', 'NCH'))
        key = jax.random.key(seed)
        ks = jax.random.split(key, 16)
        bs, n, d = (16, 1024, DIM)
        s = 0.05
        return {'x': jax.random.normal(ks[0], (bs, n, d), jnp.float32), 'mask': jnp.ones((bs, n, n), jnp.float32), 'w_se': jax.random.normal(ks[1], (3, d), jnp.float32) * s, 'b_se': jnp.zeros((3,), jnp.float32), 'conv1_w': jax.random.normal(ks[2], (d, d, 1), jnp.float32) * s, 'bn1_g': jnp.ones((d,), jnp.float32), 'bn1_b': jnp.zeros((d,), jnp.float32), 'bn1_m': jnp.zeros((d,), jnp.float32), 'bn1_v': jnp.ones((d,), jnp.float32), 'conv2_w': jax.random.normal(ks[3], (d, d, 17), jnp.float32) * s, 'bn2_g': jnp.ones((d,), jnp.float32), 'bn2_b': jnp.zeros((d,), jnp.float32), 'bn2_m': jnp.zeros((d,), jnp.float32), 'bn2_v': jnp.ones((d,), jnp.float32), 'w_msg': jax.random.normal(ks[4], (d, d), jnp.float32) * s, 'b_msg': jnp.zeros((d,), jnp.float32), 'w_ih': jax.random.normal(ks[5], (3 * d, 2 * d), jnp.float32) * s, 'b_ih': jnp.zeros((3 * d,), jnp.float32), 'w_hh': jax.random.normal(ks[6], (3 * d, d), jnp.float32) * s, 'b_hh': jnp.zeros((3 * d,), jnp.float32)}
    _L0_gnn_all = _L0_gnn_setup()
    _L0_gnn_in = {k: v for k, v in _L0_gnn_all.items() if k in ('w_se', 'b_se', 'conv1_w', 'bn1_g', 'bn1_b', 'bn1_m', 'bn1_v', 'conv2_w', 'bn2_g', 'bn2_b', 'bn2_m', 'bn2_v', 'w_msg', 'b_msg', 'w_ih', 'b_ih', 'w_hh', 'b_hh')}
    del _L0_gnn_all

    def _L0_ffn_setup():
        import jax, jax.numpy as jnp
        import numpy as np
        E = 8
        K = 2
        D = 128
        H = 256
        DOUT = 128
        EPS = 1e-05
        key = jax.random.key(seed)
        ks = jax.random.split(key, 9)
        s = 0.02
        return {'x': jax.random.normal(ks[0], (4, 4096, D), jnp.float32), 'gamma': 1.0 + 0.05 * jax.random.normal(ks[1], (D,), jnp.float32), 'beta': 0.05 * jax.random.normal(ks[2], (D,), jnp.float32), 'Wr': 0.01 * jax.random.normal(ks[3], (D, E), jnp.float32), 'br': jnp.zeros((E,), jnp.float32), 'W1': s * jax.random.normal(ks[4], (E, D, H), jnp.float32), 'b1': s * jax.random.normal(ks[5], (E, H), jnp.float32), 'W2': s * jax.random.normal(ks[6], (E, H, DOUT), jnp.float32), 'b2': s * jax.random.normal(ks[7], (E, DOUT), jnp.float32)}
    _L0_ffn_all = _L0_ffn_setup()
    _L0_ffn_in = {k: v for k, v in _L0_ffn_all.items() if k in ('gamma', 'beta', 'Wr', 'br', 'W1', 'b1', 'W2', 'b2')}
    del _L0_ffn_all
    return {'x': x, 'adj': adj, 'L0_gnn_w_se': _L0_gnn_in['w_se'], 'L0_gnn_b_se': _L0_gnn_in['b_se'], 'L0_gnn_conv1_w': _L0_gnn_in['conv1_w'], 'L0_gnn_bn1_g': _L0_gnn_in['bn1_g'], 'L0_gnn_bn1_b': _L0_gnn_in['bn1_b'], 'L0_gnn_bn1_m': _L0_gnn_in['bn1_m'], 'L0_gnn_bn1_v': _L0_gnn_in['bn1_v'], 'L0_gnn_conv2_w': _L0_gnn_in['conv2_w'], 'L0_gnn_bn2_g': _L0_gnn_in['bn2_g'], 'L0_gnn_bn2_b': _L0_gnn_in['bn2_b'], 'L0_gnn_bn2_m': _L0_gnn_in['bn2_m'], 'L0_gnn_bn2_v': _L0_gnn_in['bn2_v'], 'L0_gnn_w_msg': _L0_gnn_in['w_msg'], 'L0_gnn_b_msg': _L0_gnn_in['b_msg'], 'L0_gnn_w_ih': _L0_gnn_in['w_ih'], 'L0_gnn_b_ih': _L0_gnn_in['b_ih'], 'L0_gnn_w_hh': _L0_gnn_in['w_hh'], 'L0_gnn_b_hh': _L0_gnn_in['b_hh'], 'L0_ffn_gamma': _L0_ffn_in['gamma'], 'L0_ffn_beta': _L0_ffn_in['beta'], 'L0_ffn_Wr': _L0_ffn_in['Wr'], 'L0_ffn_br': _L0_ffn_in['br'], 'L0_ffn_W1': _L0_ffn_in['W1'], 'L0_ffn_b1': _L0_ffn_in['b1'], 'L0_ffn_W2': _L0_ffn_in['W2'], 'L0_ffn_b2': _L0_ffn_in['b2']}

def reference(x, adj, L0_gnn_w_se, L0_gnn_b_se, L0_gnn_conv1_w, L0_gnn_bn1_g, L0_gnn_bn1_b, L0_gnn_bn1_m, L0_gnn_bn1_v, L0_gnn_conv2_w, L0_gnn_bn2_g, L0_gnn_bn2_b, L0_gnn_bn2_m, L0_gnn_bn2_v, L0_gnn_w_msg, L0_gnn_b_msg, L0_gnn_w_ih, L0_gnn_b_ih, L0_gnn_w_hh, L0_gnn_b_hh, L0_ffn_gamma, L0_ffn_beta, L0_ffn_Wr, L0_ffn_br, L0_ffn_W1, L0_ffn_b1, L0_ffn_W2, L0_ffn_b2):
    import jax
    import jax.numpy as jnp

    def _L0_gnn_ref(x, mask, w_se, b_se, conv1_w, bn1_g, bn1_b, bn1_m, bn1_v, conv2_w, bn2_g, bn2_b, bn2_m, bn2_v, w_msg, b_msg, w_ih, b_ih, w_hh, b_hh):
        import jax, jax.numpy as jnp
        import numpy as np
        from jax import lax
        DIM = 128
        EPS = 1e-05

        def _bn(h, g, b, m, v):
            scale = g / jnp.sqrt(v + EPS)
            return h * scale[None, :, None] + (b - m * scale)[None, :, None]

        def _conv1d(h, w, pad):
            return lax.conv_general_dilated(h, w, window_strides=(1,), padding=[(pad, pad)], dimension_numbers=('NCH', 'OIH', 'NCH'))
        d = x.shape[-1]
        xc = jnp.transpose(x, (0, 2, 1))
        h = _bn(_conv1d(xc, conv1_w, 0), bn1_g, bn1_b, bn1_m, bn1_v)
        h = jax.nn.relu(h)
        h = _bn(_conv1d(h, conv2_w, 8), bn2_g, bn2_b, bn2_m, bn2_v)
        x_conv = jnp.transpose(jax.nn.relu(h + xc), (0, 2, 1))
        s = x @ w_se.T + b_se
        sq = jnp.sum(s * s, axis=-1)
        dist = sq[:, :, None] + sq[:, None, :] - 2.0 * jnp.einsum('bnd,bmd->bnm', s, s)
        A = jnp.exp(-dist) * mask
        msg = jax.nn.relu(x @ w_msg.T + b_msg)
        x_nmp = jnp.einsum('bnm,bmd->bnd', A, msg)
        x_in = jnp.concatenate([x_conv, x_nmp], axis=-1)
        gi = x_in @ w_ih.T + b_ih
        gh = x @ w_hh.T + b_hh
        gi_r, gi_z, gi_n = (gi[..., :d], gi[..., d:2 * d], gi[..., 2 * d:])
        gh_r, gh_z, gh_n = (gh[..., :d], gh[..., d:2 * d], gh[..., 2 * d:])
        r = jax.nn.sigmoid(gi_r + gh_r)
        z = jax.nn.sigmoid(gi_z + gh_z)
        nn_ = jnp.tanh(gi_n + r * gh_n)
        return (1.0 - z) * nn_ + z * x

    def _L0_ffn_ref(x, gamma, beta, Wr, br, W1, b1, W2, b2):
        import jax, jax.numpy as jnp
        import numpy as np
        E = 8
        K = 2
        D = 128
        H = 256
        DOUT = 128
        EPS = 1e-05
        mu = jnp.mean(x, axis=-1, keepdims=True)
        var = jnp.mean(jnp.square(x - mu), axis=-1, keepdims=True)
        xn = (x - mu) * jax.lax.rsqrt(var + EPS) * gamma + beta
        logits = jnp.einsum('bsd,de->bse', xn, Wr) + br
        top_vals, top_idx = jax.lax.top_k(logits, K)
        w = jax.nn.softmax(top_vals, axis=-1)
        w_full = jnp.einsum('bsk,bske->bse', w, jax.nn.one_hot(top_idx, E, dtype=w.dtype))
        y = jnp.zeros(x.shape[:-1] + (DOUT,), x.dtype)
        for e in range(E):
            h = jax.nn.gelu(jnp.einsum('bsd,dh->bsh', xn, W1[e]) + b1[e], approximate=False)
            y_e = jnp.einsum('bsh,hd->bsd', h, W2[e]) + b2[e]
            y = y + y_e * w_full[..., e, None]
        return y
    x = x + _L0_gnn_ref(_layernorm(x, axis=-1), adj, L0_gnn_w_se, L0_gnn_b_se, L0_gnn_conv1_w, L0_gnn_bn1_g, L0_gnn_bn1_b, L0_gnn_bn1_m, L0_gnn_bn1_v, L0_gnn_conv2_w, L0_gnn_bn2_g, L0_gnn_bn2_b, L0_gnn_bn2_m, L0_gnn_bn2_v, L0_gnn_w_msg, L0_gnn_b_msg, L0_gnn_w_ih, L0_gnn_b_ih, L0_gnn_w_hh, L0_gnn_b_hh)
    x = x + _L0_ffn_ref(_layernorm(x, axis=-1), L0_ffn_gamma, L0_ffn_beta, L0_ffn_Wr, L0_ffn_br, L0_ffn_W1, L0_ffn_b1, L0_ffn_W2, L0_ffn_b2)
    return x

_drawn_inputs = setup_inputs


def setup_inputs(seed=0):
    import zlib

    import numpy as np

    out = dict(_drawn_inputs(seed))
    spreads = {'L0_gnn_b_se': (0.0, 0.8),
     'L0_gnn_bn1_g': (1.0, 0.6),
     'L0_gnn_bn1_b': (0.0, 0.485),
     'L0_gnn_bn1_m': (0.0, 0.438),
     'L0_gnn_bn1_v': (1.0, 0.6),
     'L0_gnn_bn2_g': (1.0, 0.6),
     'L0_gnn_bn2_b': (0.0, 0.746),
     'L0_gnn_bn2_m': (0.0, 0.681),
     'L0_gnn_bn2_v': (1.0, 0.6),
     'L0_gnn_b_msg': (0.0, 0.1),
     'L0_gnn_b_ih': (0.0, 0.277),
     'L0_gnn_b_hh': (0.0, 0.384),
     'L0_ffn_br': (0.0, 0.392)}
    factors = {'L0_ffn_gamma': 8.0,
     'L0_ffn_beta': 8.0,
     'L0_ffn_Wr': 5.044,
     'L0_ffn_W1': 3.386,
     'L0_ffn_b1': 8.0,
     'L0_ffn_W2': 3.324,
     'L0_ffn_b2': 6.498}
    for name, (base, spread) in spreads.items():
        noise = np.random.default_rng([zlib.crc32(name.encode()), seed]).standard_normal(out[name].shape)
        drawn = base * np.exp(spread * noise) if base else spread * noise
        out[name] = jnp.asarray(drawn.astype(out[name].dtype))
    for name, factor in factors.items():
        out[name] = (out[name] * factor).astype(out[name].dtype)
    return out
```

```python
from contextlib import ExitStack

import numpy as np

import concourse.bass as bass
from concourse import mybir

F32 = mybir.dt.float32
F32R = mybir.dt.float32r
U32 = mybir.dt.uint32
ALU = mybir.AluOpType
ACT = mybir.ActivationFunctionType

P = 128
GRAPHS = 16
NODES = 512
NT = NODES // P
TAPS = 17
PAD = TAPS // 2
EXPERTS = 8
HALVES = 2
EPS = 1e-5
LAG = 2
PARTS = 3
SLOTS = 4
RINGS = 3

SE, CONV1, MSG = 0, 1, 2
CONV2 = 3
IH = CONV2 + TAPS
HH = IH + 6
W1 = HH + 3
W2 = W1 + 16
BLOCKS = W2 + 16
WR = BLOCKS * P
WCOLS = WR + EXPERTS
CHUNKS = [(0, 11 * P), (11 * P, IH * P), (IH * P, W1 * P), (W1 * P, W2 * P), (W2 * P, WCOLS)]
CHUNK_MAX = 17 * P
assert CHUNK_MAX >= max(b - a for a, b in CHUNKS)

K_U, K_V, K_BM, K_SEL = 0, 1, 2, 3
K_B2 = K_SEL + EXPERTS
K_BMSG = K_B2 + 1
K_BLOCKS = K_BMSG + 4
assert K_BLOCKS * P <= CHUNK_MAX

(V_G1, V_G2, V_V1, V_V2, V_B1, V_B2, V_M1, V_M2, V_IH, V_HH, V_GAMMA, V_BETA, V_SE, V_EB1, V_BR) = (
    0, 1, 2, 3, 4, 5, 6, 7, 8, 11, 14, 15, 16, 17, 33)
VCOLS = V_BR + EXPERTS
D_SC1, D_SC2, D_BI1, D_BI2, D_R, D_Z = range(6)

C_ID = 0
C_GU = C_ID + P
C_GV = C_GU + 1
C_IOTA = C_GV + 1
C_HALF = C_IOTA + EXPERTS
CCOLS = C_HALF + NT


def constants():
    c = np.zeros((P, CCOLS), np.float32)
    c[:, C_ID:C_ID + P] = np.eye(P)
    for r in range(4):
        c[32 * r:32 * r + 32, C_GU] = 0.0 if r < 2 else -1.0
        c[32 * r:32 * r + 32, C_GV] = 0.0 if r % 2 == 0 else -1.0
    c[:, C_IOTA:C_IOTA + EXPERTS] = np.arange(EXPERTS)
    c[:, C_HALF:C_HALF + NT] = -0.5
    return c


def selections():
    k = np.zeros((P, K_BLOCKS, P), np.float32)
    for r in range(4):
        for i in range(3):
            for src in (0, 32):
                k[src + i, K_U, 32 * r + i] = -2.0
                k[src + i, K_V, 32 * r + i] = 1.0
            for src in (64, 96):
                k[src + i, K_U, 32 * r + 3] = 1.0
                k[src + i, K_V, 32 * r + 4] = 1.0
        k[3, K_U, 32 * r + 4] = 1.0
        k[3, K_V, 32 * r + 3] = 1.0
    k[[0, 32], K_BM, :] = 1.0
    for e in range(EXPERTS):
        k[[e, 32 + e], K_SEL + e, :] = 1.0
    return k


def gnn_moe(nc, x, adj_t, weights, stacks, vectors, consts, out):
    x_v = x.rearrange("g (t p) d -> g p t d", p=P)
    adj_v = adj_t.rearrange("g (t p) n -> g p t n", p=P)
    out_v = out.rearrange("g (t p) d -> g p t d", p=P)

    with ExitStack() as ctx:
        def sb(name, shape, dt=F32):
            return ctx.enter_context(nc.sbuf_tensor(name, shape, dt))

        def bank(name):
            return ctx.enter_context(nc.psum_tensor(name, [P, 512], F32))

        def sem(name):
            return ctx.enter_context(nc.semaphore(name))

        w_raw = sb("w_raw", [P, 2, CHUNK_MAX])
        w_hi = sb("w_hi", [P, WCOLS], F32R)
        w_lo = sb("w_lo", [P, WCOLS], F32R)
        b2_s = sb("b2_s", [P, P], F32R)
        bm_s = sb("bm_s", [P, NODES], F32R)
        vec = sb("vec", [P, VCOLS])
        dv = sb("dv", [P, 8])
        cst = sb("cst", [P, CCOLS])
        sel = sb("sel", [P, K_BLOCKS * P], F32R)
        ge = w_raw[:, 0, 0:SLOTS * NODES].rearrange("p (s n) -> p s n", s=SLOTS)
        hw = w_raw[:, 1, 0:SLOTS * NODES].rearrange("p (s n) -> p s n", s=SLOTS)
        x_ln = sb("x_ln", [P, NT, P])
        x_res = sb("x_res", [P, NT, P])
        adj = sb("adj", [P, NT, NODES])
        st = sb("st", [P, NT, 6])
        mv = sb("mv", [P, NT, 2])
        ve = sb("ve", [P, NT])
        spare = sb("spare", [P, 2])
        rs = sb("rs", [P, NT])
        xl = sb("xl", [P, NT, P])
        xlT = sb("xlT", [P, NODES])
        xlT_h = sb("xlT_h", [P, NODES], F32R)
        xlT_l = sb("xlT_l", [P, NODES], F32R)
        h1_h = sb("h1_h", [P, NODES + 2 * PAD], F32R)
        h1_l = sb("h1_l", [P, NODES + 2 * PAD], F32R)
        s_s = sb("s_s", [P, NODES], F32R)
        u_s = sb("u_s", [P, NODES], F32R)
        v_s = sb("v_s", [P, NODES], F32R)
        msg_h = sb("msg_h", [P, NT, P], F32R)
        msg_l = sb("msg_l", [P, NT, P], F32R)
        ex = sb("ex", [P, NT, NODES])
        h1, s_f, xnT = ex[:, 0, :], ex[:, 1, :], ex[:, 2, :]
        a_h = sb("a_h", [P, NT, NODES], F32R)
        a_l = sb("a_l", [P, NT, NODES], F32R)
        xc_h = sb("xc_h", [P, NODES], F32R)
        xc_l = sb("xc_l", [P, NODES], F32R)
        nm_h = sb("nm_h", [P, NODES], F32R)
        nm_l = sb("nm_l", [P, NODES], F32R)
        tr = sb("tr", [P, NODES])
        tz = sb("tz", [P, NODES])
        gr = sb("gr", [P, NODES])
        nn = sb("nn", [P, NODES])
        xc, y_s = nn, gr
        x1 = sb("x1", [P, NT, P])
        x1_keep = sb("x1_keep", [P, NT, P])
        xn = sb("xn", [P, NT, P])
        xnT_h = sb("xnT_h", [P, NODES], F32R)
        xnT_l = sb("xnT_l", [P, NODES], F32R)
        lg = sb("lg", [P, NT, EXPERTS])
        top = sb("top", [P, NT, 8])
        top_i = sb("top_i", [P, NT, 8], U32)
        pick = sb("pick", [P, NT, 2])
        gap = sb("gap", [P, NT])
        gap_t = sb("gap_t", [P, NT])
        w12 = sb("w12", [P, NT, 2])
        hot = sb("hot", [P, NT, 2, EXPERTS])
        w_tok = sb("w_tok", [P, NT, P])
        wT_s = sb("wT_s", [P, NODES], F32R)
        hw_h = sb("hw_h", [P, RINGS * HALVES, NODES], F32R)
        hw_l = sb("hw_l", [P, RINGS * HALVES, NODES], F32R)
        o_s = sb("o_s", [P, NT, P])
        G0, G1, G2, H0, H1, WB, Y, C2 = (bank(n) for n in ("G0", "G1", "G2", "H0", "H1", "WB", "Y", "C2"))
        HB = (H0, H1)
        DIST = (H0, H1, G1, G2)

        w_loaded = [sem(f"w_loaded{i}") for i in range(len(CHUNKS))]
        vec_loaded, cst_loaded = sem("vec_loaded"), sem("cst_loaded")
        w_hi_done = sem("w_hi_done")
        w_lo_dve = sem("w_lo_dve")
        w_lo_pool = sem("w_lo_pool")
        zeroed = sem("zeroed")
        stacked = sem("stacked")
        sel_loaded, sel_done = sem("sel_loaded"), sem("sel_done")
        dv_step, dv_pow = sem("dv_step"), sem("dv_pow")
        x_ln_loaded, x_res_loaded, adj_loaded, out_stored = map(
            sem, ("x_ln_loaded", "x_res_loaded", "adj_loaded", "out_stored"))
        pe_xnT, pe_xT, pe_conv1, pe_s, pe_msg, pe_router, pe_uv, pe_dist, pe_wT, pe_conv2 = map(
            sem, ("pe_xnT", "pe_xT", "pe_conv1", "pe_s", "pe_msg", "pe_router", "pe_uv", "pe_dist", "pe_wT",
                  "pe_conv2"))
        pe_h, pe_wb, pe_y, pe_nmp, pe_r, pe_z, pe_n, pe_outT, pe_yT = map(
            sem, ("pe_h", "pe_wb", "pe_y", "pe_nmp", "pe_r", "pe_z", "pe_n", "pe_outT", "pe_yT"))
        xnT_f32, xlT_f32, h1_f32, s_f32, msg_hi, gap_tanh, uv_hi, exp_done, wT_hi = map(
            sem, ("xnT_f32", "xlT_f32", "h1_f32", "s_f32", "msg_hi", "gap_tanh", "uv_hi", "exp_done", "wT_hi"))
        gelu_done, xc_f32, nmp_hi, r_tanh, z_tanh, n_tanh, y_copied = map(
            sem, ("gelu_done", "xc_f32", "nmp_hi", "r_tanh", "z_tanh", "n_tanh", "y_copied"))
        ln1_step, xl_ready, ln2_step, xn_ready, x1_ready, x1_kept = map(
            sem, ("ln1_step", "xl_ready", "ln2_step", "xn_ready", "x1_ready", "x1_kept"))
        xnT_hi, xnT_split, xlT_hi, xlT_split, h1_hi, h1_split, s_hi, s_split, msg_split = map(
            sem, ("xnT_hi", "xnT_split", "xlT_hi", "xlT_split", "h1_hi", "h1_split", "s_hi", "s_split", "msg_split"))
        rt_step, uv_split, wT_split, a_prod, a_hi, xc_pre, xc_hi, hw_f32, hw_hi = map(
            sem, ("rt_step", "uv_split", "wT_split", "a_prod", "a_hi", "xc_pre", "xc_hi", "hw_f32", "hw_hi"))
        nmp_split, gate_step, gru_step, final_done = map(
            sem, ("nmp_split", "gate_step", "gru_step", "final_done"))
        ln1_rstd, ln2_rstd, a_split, xc_split, hw_lo = map(
            sem, ("ln1_rstd", "ln2_rstd", "a_split", "xc_split", "hw_lo"))

        def hi(block, width=P):
            return w_hi[:, block * P:block * P + width]

        def lo(block, width=P):
            return w_lo[:, block * P:block * P + width]

        def run(engine, iteration):
            iteration(0, True, False, True)
            with engine.Fori(1, GRAPHS - 1) as g:
                iteration(g, True, True, True)
            iteration(GRAPHS - 1, True, True, False)
            iteration(GRAPHS, False, True, False)

        block = ctx.enter_context(nc.Block())

        @block.sync
        def _(sp):
            sp.dma_start(x_ln[:], x_v[0]).then_inc(x_ln_loaded, 16)
            sp.dma_start(vec[:], vectors).then_inc(vec_loaded, 16)
            sp.dma_start(cst[:], consts).then_inc(cst_loaded, 16)
            sp.dma_start(w_raw[:, 1, 0:K_BLOCKS * P], stacks).then_inc(sel_loaded, 16)
            for i, (a, b) in enumerate(CHUNKS):
                if i == 1:
                    sp.wait_ge(stacked, 2)
                if 2 <= i < 4:
                    sp.wait_ge(w_lo_dve, i - 1)
                if i >= 4:
                    sp.wait_ge(w_lo_pool, i - 3)
                sp.dma_start(w_raw[:, i % 2, 0:b - a], weights[:, a:b]).then_inc(w_loaded[i], 16)
                if i == 1:
                    sp.dma_start(adj[:], adj_v[0]).then_inc(adj_loaded, 16)
                    sp.dma_start(x_res[:], x_v[0]).then_inc(x_res_loaded, 16)

            def iteration(g, gnn, ffn, more):
                f = g - 1
                if more:
                    sp.wait_ge(xl_ready, g + 1)
                    sp.dma_start(x_ln[:], x_v[g + 1]).then_inc(x_ln_loaded, 16)
                    sp.wait_ge(a_prod, NT * g + NT)
                    sp.dma_start(adj[:], adj_v[g + 1]).then_inc(adj_loaded, 16)
                    sp.wait_ge(x1_ready, g + 1)
                    sp.dma_start(x_res[:], x_v[g + 1]).then_inc(x_res_loaded, 16)
                if ffn:
                    sp.wait_ge(final_done, f + 1)
                    sp.dma_start(out_v[f], o_s[:]).then_inc(out_stored, 16)

            run(sp, iteration)
            sp.wait_ge(out_stored, 16 * GRAPHS)

        @block.tensor
        def _(pe):
            ident = cst[:, C_ID:C_ID + P]

            def product(psum, w, rhs_h, rhs_l, start=True, stop=True):
                pe.matmul(psum, hi(w), rhs_h, start=start, stop=False)
                pe.matmul(psum, hi(w), rhs_l, start=False, stop=False)
                return pe.matmul(psum, lo(w), rhs_h, start=False, stop=stop)

            def transposes(psum, tile):
                for t in range(NT):
                    last = pe.transpose(psum[:, t * P:(t + 1) * P], tile[:, t * P:(t + 1) * P], ident)
                return last

            def flat(tile):
                return tile[:, :, :].rearrange("p t d -> p (t d)")

            def conv2(g, a, b):
                for k in range(a, b):
                    last = product(C2[:], CONV2 + k, h1_h[:, k:k + NODES], h1_l[:, k:k + NODES],
                                   start=(k == 0), stop=(k == TAPS - 1))
                if b == TAPS:
                    last.then_inc(pe_conv2, 1)

            def dist(g, j):
                pe.matmul(DIST[j][:], u_s[:, j * P:(j + 1) * P], v_s[:], start=True, stop=True).then_inc(pe_dist, 1)

            def hidden(f, e):
                for h in range(HALVES):
                    if e >= 1:
                        pe.wait_ge(gelu_done, 16 * f + 2 * e - 1 + h)
                    product(HB[h][:], W1 + 2 * e + h, xnT_h[:], xnT_l[:]).then_inc(pe_h, 1)
                if e >= 1:
                    pe.wait_ge(hw_f32, 16 * f + 2 * e)
                pe.matmul(WB[:], sel[:, (K_SEL + e) * P:(K_SEL + e + 1) * P], wT_s[:],
                          start=True, stop=True).then_inc(pe_wb, 1)

            def second(f, e):
                if e == 0:
                    pe.matmul(Y[:], b2_s[:], wT_s[:], start=True, stop=False)
                for h in range(HALVES):
                    pe.wait_ge(hw_lo, 16 * f + 2 * e + h + 1)
                    slot = (e % RINGS) * HALVES + h
                    last = product(Y[:], W2 + 2 * e + h, hw_h[:, slot, :], hw_l[:, slot, :], start=False,
                                   stop=(e == EXPERTS - 1 and h == 1))
                last.then_inc(pe_y, 1)

            def iteration(g, gnn, ffn, more):
                f = g - 1
                if ffn:
                    pe.wait_ge(xn_ready, f + 1)
                    transposes(G0, flat(xn)).then_inc(pe_xnT, 1)
                if gnn:
                    pe.wait_ge(xl_ready, g + 1)
                    transposes(G1, flat(xl)).then_inc(pe_xT, 1)
                    pe.wait_ge(xlT_split, g + 1)
                    product(G2[:], CONV1, xlT_h[:], xlT_l[:]).then_inc(pe_conv1, 1)
                    product(H0[:], SE, xlT_h[:], xlT_l[:]).then_inc(pe_s, 1)
                    pe.matmul(H1[:], sel[:, K_BM * P:(K_BM + 1) * P], bm_s[:], start=True, stop=False)
                    for t in range(NT):
                        nodes = slice(t * P, (t + 1) * P)
                        pe.matmul(H1[:, nodes], xlT_h[:, nodes], hi(MSG), start=False, stop=False)
                        pe.matmul(H1[:, nodes], xlT_h[:, nodes], lo(MSG), start=False, stop=False)
                        last = pe.matmul(H1[:, nodes], xlT_l[:, nodes], hi(MSG), start=False, stop=(t == NT - 1))
                    last.then_inc(pe_msg, 1)
                if ffn:
                    pe.wait_ge(xnT_split, f + 1)
                    for t in range(NT):
                        nodes = slice(t * P, (t + 1) * P)
                        logits = G0[:, t * EXPERTS:(t + 1) * EXPERTS]
                        pe.matmul(logits, xnT_h[:, nodes], w_hi[:, WR:WCOLS], start=True, stop=False)
                        pe.matmul(logits, xnT_h[:, nodes], w_lo[:, WR:WCOLS], start=False, stop=False)
                        last = pe.matmul(logits, xnT_l[:, nodes], w_hi[:, WR:WCOLS], start=False, stop=True)
                    last.then_inc(pe_router, 1)
                if gnn:
                    pe.wait_ge(h1_split, g + 1)
                    conv2(g, 0, 8)
                    pe.wait_ge(s_split, g + 1)
                    pe.matmul(G1[:], sel[:, K_U * P:(K_U + 1) * P], s_s[:], start=True, stop=True)
                    pe.matmul(G2[:], sel[:, K_V * P:(K_V + 1) * P], s_s[:], start=True, stop=True).then_inc(pe_uv, 1)
                    conv2(g, 8, 13)
                    pe.wait_ge(uv_split, g + 1)
                    dist(g, 0)
                    pe.wait_ge(msg_split, g + 1)
                    dist(g, 1)
                if ffn:
                    pe.wait_ge(rt_step, ROUTER_STEPS * f + ROUTER_STEPS)
                    transposes(G0, flat(w_tok)).then_inc(pe_wT, 1)
                if gnn:
                    dist(g, 2)
                    dist(g, 3)
                    conv2(g, 13, TAPS)
                if ffn:
                    if gnn:
                        pe.wait_ge(exp_done, NT * g + 2)
                    pe.wait_ge(wT_split, f + 1)
                    hidden(f, 0)
                    hidden(f, 1)
                if gnn:
                    for j in range(NT):
                        pe.wait_ge(a_split, NT * g + j + 1)
                        pe.matmul(G0[:], msg_h[:, j, :], a_h[:, j, :], start=(j == 0), stop=False)
                        pe.matmul(G0[:], msg_h[:, j, :], a_l[:, j, :], start=False, stop=False)
                        last = pe.matmul(G0[:], msg_l[:, j, :], a_h[:, j, :], start=False, stop=(j == NT - 1))
                    last.then_inc(pe_nmp, 1)
                if ffn:
                    hidden(f, 2)
                    second(f, 0)
                if gnn:
                    pe.wait_ge(nmp_split, g + 1)
                    pe.wait_ge(xc_split, g + 1)
                    for gate, psum, done in ((0, G1, pe_r), (1, G2, pe_z)):
                        product(psum[:], IH + gate, xc_h[:], xc_l[:], stop=False)
                        product(psum[:], IH + 3 + gate, nm_h[:], nm_l[:], start=False, stop=False)
                        product(psum[:], HH + gate, xlT_h[:], xlT_l[:], start=False).then_inc(done, 1)
                if ffn:
                    hidden(f, 3)
                    second(f, 1)
                if gnn:
                    product(G0[:], HH + 2, xlT_h[:], xlT_l[:])
                    product(C2[:], IH + 2, xc_h[:], xc_l[:], stop=False)
                    product(C2[:], IH + 5, nm_h[:], nm_l[:], start=False).then_inc(pe_n, 1)
                if ffn:
                    for e in (4, 5, 6):
                        hidden(f, e)
                        second(f, e - LAG)
                if gnn:
                    pe.wait_ge(gru_step, 3 * g + 3)
                    for t in range(NT):
                        last = pe.transpose(G1[:, t * P:(t + 1) * P], gr[:, t * P:(t + 1) * P], ident)
                    last.then_inc(pe_outT, 1)
                if ffn:
                    hidden(f, 7)
                    second(f, 5)
                    second(f, 6)
                    second(f, 7)
                    pe.wait_ge(y_copied, f + 1)
                    for t in range(NT):
                        last = pe.transpose(G2[:, t * P:(t + 1) * P], y_s[:, t * P:(t + 1) * P], ident)
                    last.then_inc(pe_yT, 1)

            pe.wait_ge(cst_loaded, 16)
            pe.wait_ge(sel_done, 1)
            pe.wait_ge(stacked, 2)
            pe.wait_ge(zeroed, 3)
            pe.wait_ge(w_hi_done, len(CHUNKS))
            pe.wait_ge(w_lo_dve, 2)
            pe.wait_ge(w_lo_pool, len(CHUNKS) - 2)
            run(pe, iteration)

        @block.scalar
        def _(act):
            def gelu(f, e):
                for h in range(HALVES):
                    n = 2 * e + h
                    act.wait_ge(pe_h, 16 * f + n + 1)
                    if n >= SLOTS:
                        act.wait_ge(hw_f32, 16 * f + n - SLOTS + 1)
                    nc.scalar.activation(ge[:, n % SLOTS, :], HB[h][:], ACT.Gelu,
                                         bias=vec[:, V_EB1 + n:V_EB1 + n + 1]).then_inc(gelu_done, 1)

            def iteration(g, gnn, ffn, more):
                f = g - 1
                if ffn:
                    act.wait_ge(pe_xnT, f + 1)
                    nc.scalar.activation(xnT[:], G0[:], ACT.Identity, scale=vec[:, V_GAMMA:V_GAMMA + 1],
                                         bias=vec[:, V_BETA:V_BETA + 1]).then_inc(xnT_f32, 1)
                if gnn:
                    act.wait_ge(pe_xT, g + 1)
                    nc.scalar.copy(xlT[:], G1[:]).then_inc(xlT_f32, 1)
                    act.wait_ge(pe_conv1, g + 1)
                    nc.scalar.activation(h1[:], G2[:], ACT.Relu, scale=dv[:, D_SC1:D_SC1 + 1],
                                         bias=dv[:, D_BI1:D_BI1 + 1]).then_inc(h1_f32, 1)
                    act.wait_ge(pe_s, g + 1)
                    nc.scalar.activation(s_f[0:64, :], H0[0:64, :], ACT.Identity, bias=vec[0:64, V_SE:V_SE + 1])
                    nc.scalar.activation(s_f[64:P, :], H0[64:P, :], ACT.Square,
                                         bias=vec[64:P, V_SE:V_SE + 1]).then_inc(s_f32, 1)
                    act.wait_ge(pe_msg, g + 1)
                    nc.scalar.activation(msg_h[:, :, :].rearrange("p t d -> p (t d)"), H1[:],
                                         ACT.Relu).then_inc(msg_hi, 1)
                if ffn:
                    act.wait_ge(rt_step, ROUTER_STEPS * f + ROUTER_GAP)
                    nc.scalar.activation(gap_t[:], gap[:], ACT.Tanh, scale=0.5).then_inc(gap_tanh, 1)
                if gnn:
                    act.wait_ge(pe_uv, g + 1)
                    nc.scalar.copy(u_s[:], G1[:])
                    nc.scalar.copy(v_s[:], G2[:]).then_inc(uv_hi, 1)
                    for j in range(NT):
                        act.wait_ge(pe_dist, NT * g + j + 1)
                        nc.scalar.activation(ex[:, j, :], DIST[j][:], ACT.Exp, scale=-1.0).then_inc(exp_done, 1)
                        if ffn and j == 1:
                            act.wait_ge(pe_wT, f + 1)
                            nc.scalar.copy(wT_s[:], G0[:]).then_inc(wT_hi, 1)
                elif ffn:
                    act.wait_ge(pe_wT, f + 1)
                    nc.scalar.copy(wT_s[:], G0[:]).then_inc(wT_hi, 1)
                if ffn:
                    gelu(f, 0)
                if gnn:
                    act.wait_ge(xc_pre, g + 1)
                    nc.scalar.activation(xc[:], xc[:], ACT.Relu, bias=dv[:, D_BI2:D_BI2 + 1]).then_inc(xc_f32, 1)
                if ffn:
                    gelu(f, 1)
                if gnn:
                    act.wait_ge(pe_nmp, g + 1)
                    nc.scalar.copy(nm_h[:], G0[:]).then_inc(nmp_hi, 1)
                if ffn:
                    gelu(f, 2)
                if gnn:
                    act.wait_ge(pe_r, g + 1)
                    nc.scalar.activation(tr[:], G1[:], ACT.Tanh, scale=0.5,
                                         bias=dv[:, D_R:D_R + 1]).then_inc(r_tanh, 1)
                    act.wait_ge(pe_z, g + 1)
                    nc.scalar.activation(tz[:], G2[:], ACT.Tanh, scale=0.5,
                                         bias=dv[:, D_Z:D_Z + 1]).then_inc(z_tanh, 1)
                if ffn:
                    gelu(f, 3)
                    gelu(f, 4)
                if gnn:
                    act.wait_ge(gate_step, 3 * g + 3)
                    nc.scalar.activation(nn[:], tr[:], ACT.Tanh, bias=vec[:, V_IH + 2:V_IH + 3]).then_inc(n_tanh, 1)
                if ffn:
                    for e in (5, 6, 7):
                        gelu(f, e)
                    act.wait_ge(pe_y, EXPERTS * f + EXPERTS)
                    nc.scalar.copy(y_s[:], Y[:]).then_inc(y_copied, 1)

            act.wait_ge(cst_loaded, 16)
            act.wait_ge(sel_loaded, 16)
            nc.scalar.copy(sel[:], w_raw[:, 1, 0:K_BLOCKS * P]).then_inc(sel_done, 1)
            for i, (a, b) in enumerate(CHUNKS):
                act.wait_ge(w_loaded[i], 16)
                nc.scalar.copy(w_hi[:, a:b], w_raw[:, i % 2, 0:b - a]).then_inc(w_hi_done, 1)
            act.wait_ge(vec_loaded, 16)
            act.wait_ge(dv_step, 5)
            run(act, iteration)

        @block.gpsimd
        def _(pool):
            def iteration(g, gnn, ffn, more):
                f = g - 1

                def hidden_lo(e):
                    for h in range(HALVES):
                        n = 2 * e + h
                        slot = (e % RINGS) * HALVES + h
                        pool.wait_ge(hw_hi, 16 * f + n + 1)
                        nc.gpsimd.tensor_tensor(hw_l[:, slot, :], hw[:, n % SLOTS, :],
                                                hw_h[:, slot, :].bitcast(F32), ALU.subtract).then_inc(hw_lo, 1)

                if gnn:
                    for j in range(NT):
                        pool.wait_ge(a_hi, NT * g + j + 1)
                        nc.gpsimd.tensor_tensor(a_l[:, j, :], ex[:, j, :], a_h[:, j, :].bitcast(F32),
                                                ALU.subtract).then_inc(a_split, 1)
                if ffn:
                    hidden_lo(0)
                if gnn:
                    pool.wait_ge(xc_hi, g + 1)
                    nc.gpsimd.tensor_tensor(xc_l[:], xc[:], xc_h[:].bitcast(F32), ALU.subtract).then_inc(xc_split, 1)
                if ffn:
                    for e in (1, 2, 3, 4):
                        hidden_lo(e)
                if more:
                    pool.wait_ge(ln1_step, 3 * g + 6)
                    nc.gpsimd.tensor_tensor(rs[:], ve[:], cst[:, C_HALF:C_HALF + NT], ALU.pow).then_inc(ln1_rstd, 1)
                if ffn:
                    for e in (5, 6):
                        hidden_lo(e)
                if gnn:
                    pool.wait_ge(ln2_step, 3 * g + 3)
                    nc.gpsimd.tensor_tensor(rs[:], ve[:], cst[:, C_HALF:C_HALF + NT], ALU.pow).then_inc(ln2_rstd, 1)
                if ffn:
                    hidden_lo(7)

            for tile in (h1_h, h1_l):
                nc.gpsimd.memset(tile[:, 0:PAD].bitcast(F32), 0.0)
                nc.gpsimd.memset(tile[:, PAD + NODES:].bitcast(F32), 0.0).then_inc(zeroed, 1)
            nc.gpsimd.memset(w_tok[:], 0.0).then_inc(zeroed, 1)
            pool.wait_ge(cst_loaded, 16)
            pool.wait_ge(dv_step, 1)
            nc.gpsimd.tensor_tensor(dv[:, 6:8], dv[:, 6:8], cst[:, C_HALF:C_HALF + 2], ALU.pow).then_inc(dv_pow, 1)
            pool.wait_ge(ln1_step, 3)
            nc.gpsimd.tensor_tensor(rs[:], ve[:], cst[:, C_HALF:C_HALF + NT], ALU.pow).then_inc(ln1_rstd, 1)
            for i in range(2, len(CHUNKS)):
                a, b = CHUNKS[i]
                pool.wait_ge(w_hi_done, i + 1)
                nc.gpsimd.tensor_tensor(w_lo[:, a:b], w_raw[:, i % 2, 0:b - a], w_hi[:, a:b].bitcast(F32),
                                        ALU.subtract).then_inc(w_lo_pool, 1)
            run(pool, iteration)

        @block.vector
        def _(dve):
            def v2(tile):
                return tile[:, :, :].rearrange("p t d -> p (t d)")

            def split(src, dst_h, dst_l, hi_done, lo_done, g):
                nc.vector.tensor_copy(dst_h, src).then_inc(hi_done, 1)
                dve.wait_ge(hi_done, g + 1)
                nc.vector.tensor_tensor(dst_l, src, dst_h.bitcast(F32), ALU.subtract).then_inc(lo_done, 1)

            def carry_wait():
                nc.vector.memset(spare[:], 0.0)

            def statistics(src, step, g, scale, bias):
                for t in range(NT):
                    last = nc.vector.bn_stats(st[:, t, :], src[:, t, :])
                last.then_inc(step, 1)
                dve.wait_ge(step, 3 * g + 1)
                carry_wait()
                for t in range(NT):
                    last = nc.vector.bn_aggr(mv[:, t, :], st[:, t, :])
                last.then_inc(step, 1)
                dve.wait_ge(step, 3 * g + 2)
                nc.vector.tensor_scalar(ve[:], mv[:, :, 1], scale, bias, ALU.mult, ALU.add).then_inc(step, 1)

            def normalize(dst, src, rstd_done, ready, g):
                dve.wait_ge(rstd_done, g + 1)
                for t in range(NT):
                    last = nc.vector.tensor_scalar(dst[:, t, :], src[:, t, :], mv[:, t, 0:1], rs[:, t:t + 1],
                                                   ALU.subtract, ALU.mult)
                last.then_inc(ready, 1)

            def first_norm(g):
                dve.wait_ge(x_ln_loaded, 16 * g + 16)
                statistics(x_ln, ln1_step, g, 1.0, EPS)
                normalize(xl, x_ln, ln1_rstd, xl_ready, g)

            def router(f):
                done = [0]

                def step(instruction):
                    done[0] += 1
                    instruction.then_inc(rt_step, 1)
                    dve.wait_ge(rt_step, ROUTER_STEPS * f + done[0])

                dve.wait_ge(pe_router, f + 1)
                br = vec[:, V_BR:V_BR + EXPERTS].unsqueeze(1).broadcast_to([P, NT, EXPERTS])
                step(nc.vector.tensor_tensor(lg[:], G0[:, 0:NT * EXPERTS].rearrange("p (t e) -> p t e", t=NT), br,
                                             ALU.add))
                carry_wait()
                for t in range(NT):
                    last = nc.vector.max(top[:, t, :], lg[:, t, :])
                step(last)
                nc.vector.tensor_tensor(gap[:], top[:, :, 0], top[:, :, 1], ALU.subtract).then_inc(rt_step, 1)
                done[0] += 1
                assert done[0] == ROUTER_GAP
                for t in range(NT):
                    last = nc.vector.max_index(top_i[:, t, :], top[:, t, :], lg[:, t, :])
                step(last)
                step(nc.vector.tensor_copy(pick[:], top_i[:, :, 0:2]))
                iota = cst[:, C_IOTA:C_IOTA + EXPERTS].unsqueeze(1).broadcast_to([P, NT * 2, EXPERTS])
                hots = hot[:, :, :, :].rearrange("p t k e -> p (t k) e")
                picks = pick[:, :, :].rearrange("p t k -> p (t k)").unsqueeze(2).broadcast_to([P, NT * 2, EXPERTS])
                nc.vector.tensor_tensor(hots, iota, picks, ALU.is_equal)
                dve.wait_ge(gap_tanh, f + 1)
                nc.vector.tensor_scalar(w12[:, :, 0], gap_t[:], 0.5, 0.5, ALU.mult, ALU.add)
                step(nc.vector.tensor_scalar(w12[:, :, 1], gap_t[:], -0.5, 0.5, ALU.mult, ALU.add))
                w12s = w12[:, :, :].rearrange("p t k -> p (t k)").unsqueeze(2).broadcast_to([P, NT * 2, EXPERTS])
                step(nc.vector.tensor_tensor(hots, hots, w12s, ALU.mult))
                for r in range(4):
                    last = nc.vector.tensor_tensor(w_tok[:, :, 32 * r:32 * r + EXPERTS], hot[:, :, 0, :],
                                                   hot[:, :, 1, :], ALU.add)
                step(last)
                assert done[0] == ROUTER_STEPS

            def weigh(f, e):
                for h in range(HALVES):
                    n = 2 * e + h
                    dve.wait_ge(gelu_done, 16 * f + n + 1)
                    if h == 0:
                        dve.wait_ge(pe_wb, EXPERTS * f + e + 1)
                    if n >= SLOTS:
                        dve.wait_ge(hw_lo, 16 * f + n - SLOTS + 1)
                    nc.vector.tensor_tensor(hw[:, n % SLOTS, :], ge[:, n % SLOTS, :], WB[:],
                                            ALU.mult).then_inc(hw_f32, 1)
                for h in range(HALVES):
                    n = 2 * e + h
                    dve.wait_ge(hw_f32, 16 * f + n + 1)
                    if e >= RINGS and h == 0:
                        dve.wait_ge(pe_y, EXPERTS * f + e - RINGS + 1)
                    nc.vector.tensor_copy(hw_h[:, (e % RINGS) * HALVES + h, :], hw[:, n % SLOTS, :]
                                          ).then_inc(hw_hi, 1)

            def iteration(g, gnn, ffn, more):
                f = g - 1
                if ffn:
                    dve.wait_ge(xnT_f32, f + 1)
                    split(xnT[:], xnT_h[:], xnT_l[:], xnT_hi, xnT_split, f)
                    nc.vector.tensor_copy(x1_keep[:], x1[:]).then_inc(x1_kept, 1)
                if gnn:
                    dve.wait_ge(xlT_f32, g + 1)
                    split(xlT[:], xlT_h[:], xlT_l[:], xlT_hi, xlT_split, g)
                    dve.wait_ge(h1_f32, g + 1)
                    split(h1[:], h1_h[:, PAD:PAD + NODES], h1_l[:, PAD:PAD + NODES], h1_hi, h1_split, g)
                    dve.wait_ge(s_f32, g + 1)
                    nc.vector.tensor_copy(s_s[:], s_f[:]).then_inc(s_hi, 1)
                    dve.wait_ge(s_hi, g + 1)
                    nc.vector.scalar_tensor_tensor(out=s_s[:], in0=s_s[:].bitcast(F32), scalar=cst[:, C_GV:C_GV + 1],
                                                   in1=s_f[:], op0=ALU.mult, op1=ALU.add).then_inc(s_split, 1)
                    dve.wait_ge(msg_hi, g + 1)
                    nc.vector.scalar_tensor_tensor(out=v2(msg_l), in0=H1[:], scalar=0.0,
                                                   in1=v2(msg_h).bitcast(F32), op0=ALU.max,
                                                   op1=ALU.subtract).then_inc(msg_split, 1)
                if ffn:
                    router(f)
                if gnn:
                    dve.wait_ge(uv_hi, g + 1)
                    nc.vector.scalar_tensor_tensor(out=u_s[:], in0=u_s[:].bitcast(F32), scalar=cst[:, C_GU:C_GU + 1],
                                                   in1=G1[:], op0=ALU.mult, op1=ALU.add)
                    nc.vector.scalar_tensor_tensor(out=v_s[:], in0=v_s[:].bitcast(F32), scalar=cst[:, C_GV:C_GV + 1],
                                                   in1=G2[:], op0=ALU.mult, op1=ALU.add).then_inc(uv_split, 1)
                if ffn:
                    dve.wait_ge(wT_hi, f + 1)
                    nc.vector.scalar_tensor_tensor(out=wT_s[:], in0=wT_s[:].bitcast(F32), scalar=cst[:, C_GV:C_GV + 1],
                                                   in1=G0[:], op0=ALU.mult, op1=ALU.add).then_inc(wT_split, 1)
                if gnn:
                    dve.wait_ge(adj_loaded, 16 * g + 16)
                    for j in range(NT):
                        dve.wait_ge(exp_done, NT * g + j + 1)
                        nc.vector.tensor_tensor(ex[:, j, :], ex[:, j, :], adj[:, j, :], ALU.mult).then_inc(a_prod, 1)
                        dve.wait_ge(a_prod, NT * g + j + 1)
                        nc.vector.tensor_copy(a_h[:, j, :], ex[:, j, :]).then_inc(a_hi, 1)
                    dve.wait_ge(pe_conv2, g + 1)
                    nc.vector.scalar_tensor_tensor(out=xc[:], in0=C2[:], scalar=dv[:, D_SC2:D_SC2 + 1], in1=xlT[:],
                                                   op0=ALU.mult, op1=ALU.add).then_inc(xc_pre, 1)
                if ffn:
                    weigh(f, 0)
                if gnn:
                    dve.wait_ge(xc_f32, g + 1)
                    nc.vector.tensor_copy(xc_h[:], xc[:]).then_inc(xc_hi, 1)
                if ffn:
                    weigh(f, 1)
                if gnn:
                    dve.wait_ge(nmp_hi, g + 1)
                    nc.vector.tensor_tensor(nm_l[:], G0[:], nm_h[:].bitcast(F32), ALU.subtract).then_inc(nmp_split, 1)
                if ffn:
                    weigh(f, 2)
                    weigh(f, 3)
                if gnn:
                    dve.wait_ge(r_tanh, g + 1)
                    nc.vector.tensor_scalar(tr[:], tr[:], 0.5, 0.5, ALU.mult, ALU.add).then_inc(gate_step, 1)
                    dve.wait_ge(pe_n, g + 1)
                    dve.wait_ge(gate_step, 3 * g + 1)
                    nc.vector.scalar_tensor_tensor(out=tr[:], in0=G0[:], scalar=vec[:, V_HH + 2:V_HH + 3], in1=tr[:],
                                                   op0=ALU.add, op1=ALU.mult).then_inc(gate_step, 1)
                    dve.wait_ge(gate_step, 3 * g + 2)
                    nc.vector.tensor_tensor(tr[:], tr[:], C2[:], ALU.add).then_inc(gate_step, 1)
                if ffn:
                    weigh(f, 4)
                if more:
                    first_norm(g + 1)
                if ffn:
                    weigh(f, 5)
                if gnn:
                    dve.wait_ge(n_tanh, g + 1)
                    nc.vector.tensor_tensor(gr[:], xlT[:], nn[:], ALU.subtract).then_inc(gru_step, 1)
                    dve.wait_ge(z_tanh, g + 1)
                    dve.wait_ge(gru_step, 3 * g + 1)
                    nc.vector.scalar_tensor_tensor(out=gr[:], in0=tz[:], scalar=1.0, in1=gr[:], op0=ALU.add,
                                                   op1=ALU.mult).then_inc(gru_step, 1)
                    dve.wait_ge(gru_step, 3 * g + 2)
                    nc.vector.scalar_tensor_tensor(out=gr[:], in0=gr[:], scalar=0.5, in1=nn[:], op0=ALU.mult,
                                                   op1=ALU.add).then_inc(gru_step, 1)
                if ffn:
                    weigh(f, 6)
                if gnn:
                    dve.wait_ge(pe_outT, g + 1)
                    dve.wait_ge(x_res_loaded, 16 * g + 16)
                    nc.vector.tensor_tensor(v2(x1), v2(x_res), G1[:], ALU.add).then_inc(x1_ready, 1)
                    dve.wait_ge(x1_ready, g + 1)
                    statistics(x1, ln2_step, g, 1.0 + EPS, EPS * EPS)
                    normalize(xn, x1, ln2_rstd, xn_ready, g)
                if ffn:
                    weigh(f, 7)
                    dve.wait_ge(pe_yT, f + 1)
                    dve.wait_ge(x1_kept, f + 1)
                    if not isinstance(g, int) or f >= 1:
                        dve.wait_ge(out_stored, 16 * f)
                    nc.vector.tensor_tensor(v2(o_s), v2(x1_keep), G2[:], ALU.add).then_inc(final_done, 1)

            dve.wait_ge(vec_loaded, 16)
            nc.vector.tensor_scalar(dv[:, 6:8], vec[:, V_V1:V_V2 + 1], EPS, None, ALU.add).then_inc(dv_step, 1)
            nc.vector.tensor_tensor(dv[:, D_R:D_Z + 1], vec[:, V_IH:V_IH + 2], vec[:, V_HH:V_HH + 2],
                                    ALU.add).then_inc(dv_step, 1)
            dve.wait_ge(dv_step, 2)
            nc.vector.tensor_scalar(dv[:, D_R:D_Z + 1], dv[:, D_R:D_Z + 1], 0.5, None, ALU.mult)
            dve.wait_ge(dv_pow, 1)
            nc.vector.tensor_tensor(dv[:, D_SC1:D_SC2 + 1], vec[:, V_G1:V_G2 + 1], dv[:, 6:8],
                                    ALU.mult).then_inc(dv_step, 1)
            dve.wait_ge(dv_step, 3)
            nc.vector.tensor_tensor(dv[:, D_BI1:D_BI2 + 1], vec[:, V_M1:V_M2 + 1], dv[:, D_SC1:D_SC2 + 1],
                                    ALU.mult).then_inc(dv_step, 1)
            dve.wait_ge(dv_step, 4)
            nc.vector.tensor_tensor(dv[:, D_BI1:D_BI2 + 1], vec[:, V_B1:V_B2 + 1], dv[:, D_BI1:D_BI2 + 1],
                                    ALU.subtract).then_inc(dv_step, 1)
            dve.wait_ge(cst_loaded, 16)
            first_norm(0)
            dve.wait_ge(sel_done, 1)
            for dst, first, width, pattern in ((b2_s, K_B2, P, C_GU), (bm_s, K_BMSG, NODES, C_GV)):
                cols = slice(first * P, first * P + width)
                nc.vector.scalar_tensor_tensor(out=dst[:], in0=sel[:, cols].bitcast(F32),
                                               scalar=cst[:, pattern:pattern + 1], in1=w_raw[:, 1, cols],
                                               op0=ALU.mult, op1=ALU.add).then_inc(stacked, 1)
            for i in range(2):
                a, b = CHUNKS[i]
                dve.wait_ge(w_hi_done, i + 1)
                nc.vector.tensor_tensor(w_lo[:, a:b], w_raw[:, i, 0:b - a], w_hi[:, a:b].bitcast(F32),
                                        ALU.subtract).then_inc(w_lo_dve, 1)
            run(dve, iteration)


ROUTER_GAP = 3
ROUTER_STEPS = 8


def kernel(**inputs):
    import concourse.bacc as bacc
    from concourse.bass_utils import run_bass_kernel_spmd

    a = {k: np.asarray(v) for k, v in inputs.items()}
    g = {k.removeprefix("L0_gnn_"): v for k, v in a.items()}
    e = {k.removeprefix("L0_ffn_"): v for k, v in a.items()}

    w = np.zeros((P, WCOLS), np.float32)
    k = selections()

    def put(block, value):
        w[:value.shape[0], block * P:block * P + value.shape[1]] = value

    for r in range(4):
        w[:, SE * P + 32 * r:SE * P + 32 * r + 3] = g["w_se"].T
        k[32 * r:32 * r + EXPERTS, K_B2] = e["b2"]
    put(CONV1, g["conv1_w"][:, :, 0].T)
    put(MSG, g["w_msg"].T)
    for row in (0, 32):
        for t in range(NT):
            k[row, K_BMSG + t] = g["b_msg"]
    for tap in range(TAPS):
        put(CONV2 + tap, g["conv2_w"][:, :, tap].T)
    for gate in range(3):
        rows = slice(gate * P, (gate + 1) * P)
        put(IH + gate, g["w_ih"][rows, 0:P].T)
        put(IH + 3 + gate, g["w_ih"][rows, P:2 * P].T)
        put(HH + gate, g["w_hh"][rows].T)
    for n in range(EXPERTS):
        for h in range(HALVES):
            half = slice(h * P, (h + 1) * P)
            put(W1 + 2 * n + h, e["W1"][n][:, half])
            put(W2 + 2 * n + h, e["W2"][n][half, :])
    w[:, WR:WCOLS] = e["Wr"]

    v = np.zeros((P, VCOLS), np.float32)
    for col, name in ((V_G1, "bn1_g"), (V_G2, "bn2_g"), (V_V1, "bn1_v"), (V_V2, "bn2_v"), (V_B1, "bn1_b"),
                      (V_B2, "bn2_b"), (V_M1, "bn1_m"), (V_M2, "bn2_m")):
        v[:, col] = g[name]
    for gate in range(3):
        v[:, V_IH + gate] = g["b_ih"][gate * P:(gate + 1) * P]
        v[:, V_HH + gate] = g["b_hh"][gate * P:(gate + 1) * P]
    v[:, V_GAMMA] = e["gamma"]
    v[:, V_BETA] = e["beta"]
    for r in range(4):
        v[32 * r:32 * r + 3, V_SE] = g["b_se"]
        v[32 * r + 3, V_SE] = 1.0
    for n in range(EXPERTS):
        for h in range(HALVES):
            v[:, V_EB1 + 2 * n + h] = e["b1"][n, h * P:(h + 1) * P]
    v[:, V_BR:V_BR + EXPERTS] = e["br"]

    arrays = {
        "x": np.ascontiguousarray(a["x"]),
        "adj_t": np.ascontiguousarray(a["adj"].transpose(0, 2, 1)),
        "weights": w,
        "stacks": k.reshape(P, K_BLOCKS * P),
        "vectors": v,
        "consts": constants(),
    }
    nc = bacc.Bacc("TRN2", target_bir_lowering=False, num_devices=1)
    args = [nc.dram_tensor(n, t.shape, F32, kind="ExternalInput").ap() for n, t in arrays.items()]
    out = nc.dram_tensor("out", a["x"].shape, F32, kind="ExternalOutput").ap()
    gnn_moe(nc, *args, out)
    result = run_bass_kernel_spmd(nc, [arrays], core_ids=[0])
    return result.results[0]["out"]
```

```python
from contextlib import ExitStack

import numpy as np

import concourse.bass as bass
from concourse import mybir

F32 = mybir.dt.float32
F32R = mybir.dt.float32r
U32 = mybir.dt.uint32
ALU = mybir.AluOpType
ACT = mybir.ActivationFunctionType

P = 128
GRAPHS = 16
NODES = 512
NT = NODES // P
TAPS = 17
PAD = TAPS // 2
EXPERTS = 8
HALVES = 2
EPS = 1e-5
LAG = 2
PARTS = 3
SLOTS = 4
RINGS = 3

SE, CONV1, MSG = 0, 1, 2
CONV2 = 3
IH = CONV2 + TAPS
HH = IH + 6
W1 = HH + 3
W2 = W1 + 16
BLOCKS = W2 + 16
WCOLS = BLOCKS * P
CHUNKS = [(0, 11 * P), (11 * P, IH * P), (IH * P, W1 * P), (W1 * P, W2 * P), (W2 * P, WCOLS)]
CHUNK_MAX = 17 * P
assert CHUNK_MAX >= max(b - a for a, b in CHUNKS)

K_U, K_V, K_SEL = 0, 1, 2
K_B2 = K_SEL + EXPERTS
K_BLOCKS = K_B2 + 1
assert K_BLOCKS * P <= CHUNK_MAX

(V_G1, V_G2, V_V1, V_V2, V_B1, V_B2, V_M1, V_M2, V_IH, V_HH, V_GAMMA, V_BETA, V_SE, V_EB1, V_BR, V_BM,
 V_WR) = (0, 1, 2, 3, 4, 5, 6, 7, 8, 11, 14, 15, 16, 17, 33, 34, 35)
VCOLS = V_WR + EXPERTS
D_SC1, D_SC2, D_BI1, D_BI2, D_R, D_Z = range(6)

C_ID = 0
C_GU = C_ID + P
C_GV = C_GU + 1
C_IOTA = C_GV + 1
C_HALF = C_IOTA + EXPERTS
CCOLS = C_HALF + NT


def constants():
    c = np.zeros((P, CCOLS), np.float32)
    c[:, C_ID:C_ID + P] = np.eye(P)
    for r in range(4):
        c[32 * r:32 * r + 32, C_GU] = 0.0 if r < 2 else -1.0
        c[32 * r:32 * r + 32, C_GV] = 0.0 if r % 2 == 0 else -1.0
    c[:, C_IOTA:C_IOTA + EXPERTS] = np.arange(EXPERTS)
    c[:, C_HALF:C_HALF + NT] = -0.5
    return c


def selections():
    k = np.zeros((P, K_BLOCKS, P), np.float32)
    for r in range(4):
        for i in range(3):
            for src in (0, 32):
                k[src + i, K_U, 32 * r + i] = -2.0
                k[src + i, K_V, 32 * r + i] = 1.0
            for src in (64, 96):
                k[src + i, K_U, 32 * r + 3] = 1.0
                k[src + i, K_V, 32 * r + 4] = 1.0
        k[3, K_U, 32 * r + 4] = 1.0
        k[3, K_V, 32 * r + 3] = 1.0
    for e in range(EXPERTS):
        k[[e, 32 + e], K_SEL + e, :] = 1.0
    return k


def gnn_moe(nc, x, adj_t, weights, stacks, vectors, consts, out):
    x_v = x.rearrange("g (t p) d -> g p t d", p=P)
    adj_v = adj_t.rearrange("g (t p) n -> g p t n", p=P)
    out_v = out.rearrange("g (t p) d -> g p t d", p=P)

    with ExitStack() as ctx:
        def sb(name, shape, dt=F32):
            return ctx.enter_context(nc.sbuf_tensor(name, shape, dt))

        def bank(name):
            return ctx.enter_context(nc.psum_tensor(name, [P, 512], F32))

        def sem(name):
            return ctx.enter_context(nc.semaphore(name))

        w_raw = sb("w_raw", [P, 2, CHUNK_MAX])
        w_hi = sb("w_hi", [P, WCOLS], F32R)
        w_lo = sb("w_lo", [P, WCOLS], F32R)
        b2_s = sb("b2_s", [P, P], F32R)
        vec = sb("vec", [P, VCOLS])
        dv = sb("dv", [P, 8])
        cst = sb("cst", [P, CCOLS])
        sel = sb("sel", [P, K_BLOCKS * P], F32R)
        ge = w_raw[:, 0, 0:SLOTS * NODES].rearrange("p (s n) -> p s n", s=SLOTS)
        hw = w_raw[:, 1, 0:SLOTS * NODES].rearrange("p (s n) -> p s n", s=SLOTS)
        x_ln = sb("x_ln", [P, NT, P])
        x_res = sb("x_res", [P, NT, P])
        adj = sb("adj", [P, NT, NODES])
        st = sb("st", [P, NT, 6])
        mv = sb("mv", [P, NT, 2])
        ve = sb("ve", [P, NT])
        spare = sb("spare", [P, 2])
        rs = sb("rs", [P, NT])
        xl = sb("xl", [P, NT, P])
        xlT = sb("xlT", [P, NODES])
        xlT_keep = sb("xlT_keep", [P, NODES])
        xlT_h = sb("xlT_h", [P, NODES], F32R)
        xlT_l = sb("xlT_l", [P, NODES], F32R)
        h1_h = sb("h1_h", [P, NODES + 2 * PAD], F32R)
        h1_l = sb("h1_l", [P, NODES + 2 * PAD], F32R)
        s_s = sb("s_s", [P, NODES], F32R)
        u_s = sb("u_s", [P, NODES], F32R)
        v_s = sb("v_s", [P, NODES], F32R)
        msg_h = sb("msg_h", [P, NT, P], F32R)
        msg_l = sb("msg_l", [P, NT, P], F32R)
        ex = sb("ex", [P, NT, NODES])
        h1, s_f, msg_f, y_s = (ex[:, j, :] for j in range(NT))
        a_h = sb("a_h", [P, NT, NODES], F32R)
        a_l = sb("a_l", [P, NT, NODES], F32R)
        xc_h = sb("xc_h", [P, NODES], F32R)
        xc_l = sb("xc_l", [P, NODES], F32R)
        nm_h = sb("nm_h", [P, NODES], F32R)
        nm_l = sb("nm_l", [P, NODES], F32R)
        tr = sb("tr", [P, NODES])
        tz = sb("tz", [P, NODES])
        gr = sb("gr", [P, NODES])
        nn = sb("nn", [P, NODES])
        xc, lgT = nn, tr
        x1 = sb("x1", [P, NT, P])
        x1_keep = sb("x1_keep", [P, NT, P])
        xn = sb("xn", [P, NT, P])
        xnT = sb("xnT", [P, NODES])
        xnT_h = sb("xnT_h", [P, NODES], F32R)
        xnT_l = sb("xnT_l", [P, NODES], F32R)
        lg = sb("lg", [P, NT, EXPERTS])
        top = sb("top", [P, NT, 8])
        top_i = sb("top_i", [P, NT, 8], U32)
        pick = sb("pick", [P, NT, 2])
        gap = sb("gap", [P, NT])
        gap_t = sb("gap_t", [P, NT])
        w12 = sb("w12", [P, NT, 2])
        hot = sb("hot", [P, NT, 2, EXPERTS])
        w_tok = sb("w_tok", [P, NT, P])
        wT_s = sb("wT_s", [P, NODES], F32R)
        hw_h = sb("hw_h", [P, RINGS * HALVES, NODES], F32R)
        hw_l = sb("hw_l", [P, RINGS * HALVES, NODES], F32R)
        o_s = sb("o_s", [P, NT, P])
        G0, G1, G2, H0, H1, WB, Y, C2 = (bank(n) for n in ("G0", "G1", "G2", "H0", "H1", "WB", "Y", "C2"))
        HB = (H0, H1)
        DIST = (G1, G2, G1, G2)

        w_loaded = [sem(f"w_loaded{i}") for i in range(len(CHUNKS))]
        vec_loaded, cst_loaded = sem("vec_loaded"), sem("cst_loaded")
        w_hi_done = sem("w_hi_done")
        w_lo_dve = sem("w_lo_dve")
        w_lo_pool = sem("w_lo_pool")
        zeroed = sem("zeroed")
        stacked = sem("stacked")
        sel_loaded, sel_done = sem("sel_loaded"), sem("sel_done")
        dv_step, dv_pow = sem("dv_step"), sem("dv_pow")
        x_ln_loaded, x_res_loaded, adj_loaded, out_stored = map(
            sem, ("x_ln_loaded", "x_res_loaded", "adj_loaded", "out_stored"))
        pe_xnT, pe_xT, pe_conv1, pe_s, pe_msg, pe_router, pe_uv, pe_dist, pe_wT, pe_conv2, pe_msgT, pe_lgT = map(
            sem, ("pe_xnT", "pe_xT", "pe_conv1", "pe_s", "pe_msg", "pe_router", "pe_uv", "pe_dist", "pe_wT",
                  "pe_conv2", "pe_msgT", "pe_lgT"))
        pe_h, pe_wb, pe_y, pe_nmp, pe_r, pe_z, pe_n, pe_outT, pe_yT = map(
            sem, ("pe_h", "pe_wb", "pe_y", "pe_nmp", "pe_r", "pe_z", "pe_n", "pe_outT", "pe_yT"))
        xnT_f32, xlT_f32, h1_f32, s_f32, msg_f32, msg_hi, lgT_f32, gap_tanh, uv_hi, exp_done, wT_hi = map(
            sem, ("xnT_f32", "xlT_f32", "h1_f32", "s_f32", "msg_f32", "msg_hi", "lgT_f32", "gap_tanh", "uv_hi",
                  "exp_done", "wT_hi"))
        gelu_done, hw_hi, xc_f32, nmp_hi, r_tanh, z_tanh, n_tanh, y_copied = map(
            sem, ("gelu_done", "hw_hi", "xc_f32", "nmp_hi", "r_tanh", "z_tanh", "n_tanh", "y_copied"))
        ln1_step, xl_ready, ln2_step, xn_ready, x1_ready, x1_kept = map(
            sem, ("ln1_step", "xl_ready", "ln2_step", "xn_ready", "x1_ready", "x1_kept"))
        xnT_hi, xnT_split, xlT_hi, xlT_split, h1_hi, h1_split, s_hi, s_split, msg_split = map(
            sem, ("xnT_hi", "xnT_split", "xlT_hi", "xlT_split", "h1_hi", "h1_split", "s_hi", "s_split", "msg_split"))
        xlT_kept, rt_step, uv_split, wT_split, a_prod, a_hi, xc_pre, xc_hi, hw_f32 = map(
            sem, ("xlT_kept", "rt_step", "uv_split", "wT_split", "a_prod", "a_hi", "xc_pre", "xc_hi", "hw_f32"))
        nmp_split, gate_step, gru_step, final_done = map(
            sem, ("nmp_split", "gate_step", "gru_step", "final_done"))
        ln1_rstd, ln2_rstd, a_split, xc_split, hw_lo = map(
            sem, ("ln1_rstd", "ln2_rstd", "a_split", "xc_split", "hw_lo"))

        def hi(block, width=P):
            return w_hi[:, block * P:block * P + width]

        def lo(block, width=P):
            return w_lo[:, block * P:block * P + width]

        def run(engine, iteration):
            iteration(0, True, False, False, True)
            iteration(1, True, True, False, True)
            with engine.Fori(2, GRAPHS - 1) as g:
                iteration(g, True, True, True, True)
            iteration(GRAPHS - 1, True, True, True, False)
            iteration(GRAPHS, False, True, True, False)
            iteration(GRAPHS + 1, False, False, True, False)

        block = ctx.enter_context(nc.Block())

        @block.sync
        def _(sp):
            sp.dma_start(x_ln[:], x_v[0]).then_inc(x_ln_loaded, 16)
            sp.dma_start(vec[:], vectors).then_inc(vec_loaded, 16)
            sp.dma_start(cst[:], consts).then_inc(cst_loaded, 16)
            sp.dma_start(w_raw[:, 1, 0:K_BLOCKS * P], stacks).then_inc(sel_loaded, 16)
            for i, (a, b) in enumerate(CHUNKS):
                if i == 1:
                    sp.wait_ge(stacked, 1)
                if 2 <= i < 4:
                    sp.wait_ge(w_lo_dve, i - 1)
                if i >= 4:
                    sp.wait_ge(w_lo_pool, i - 3)
                sp.dma_start(w_raw[:, i % 2, 0:b - a], weights[:, a:b]).then_inc(w_loaded[i], 16)
                if i == 1:
                    sp.dma_start(adj[:], adj_v[0]).then_inc(adj_loaded, 16)

            def iteration(g, gnn, tail, ffn, more):
                d, f = g - 1, g - 2
                if more:
                    sp.wait_ge(xl_ready, g + 1)
                    sp.dma_start(x_ln[:], x_v[g + 1]).then_inc(x_ln_loaded, 16)
                    sp.wait_ge(a_prod, NT * g + NT)
                    sp.dma_start(adj[:], adj_v[g + 1]).then_inc(adj_loaded, 16)
                if ffn:
                    sp.wait_ge(final_done, f + 1)
                    sp.dma_start(out_v[f], o_s[:]).then_inc(out_stored, 16)
                    sp.wait_ge(out_stored, 16 * f + 16)
                if gnn:
                    if tail:
                        sp.wait_ge(x1_ready, d + 1)
                    sp.dma_start(x_res[:], x_v[g]).then_inc(x_res_loaded, 16)

            run(sp, iteration)

        @block.tensor
        def _(pe):
            ident = cst[:, C_ID:C_ID + P]

            def product(psum, w, rhs_h, rhs_l, start=True, stop=True):
                pe.matmul(psum, hi(w), rhs_h, start=start, stop=False)
                pe.matmul(psum, hi(w), rhs_l, start=False, stop=False)
                return pe.matmul(psum, lo(w), rhs_h, start=False, stop=stop)

            def transposes(psum, tile):
                for t in range(NT):
                    last = pe.transpose(psum[:, t * P:(t + 1) * P], tile[:, t * P:(t + 1) * P], ident)
                return last

            def flat(tile):
                return tile[:, :, :].rearrange("p t d -> p (t d)")

            def conv2(a, b):
                for k in range(a, b):
                    last = product(C2[:], CONV2 + k, h1_h[:, k:k + NODES], h1_l[:, k:k + NODES],
                                   start=(k == 0), stop=(k == TAPS - 1))
                if b == TAPS:
                    last.then_inc(pe_conv2, 1)

            def dist(j):
                pe.matmul(DIST[j][:], u_s[:, j * P:(j + 1) * P], v_s[:], start=True, stop=True).then_inc(pe_dist, 1)

            def hidden(f, e):
                for h in range(HALVES):
                    if e >= 1:
                        pe.wait_ge(gelu_done, 16 * f + 2 * e - 1 + h)
                    product(HB[h][:], W1 + 2 * e + h, xnT_h[:], xnT_l[:]).then_inc(pe_h, 1)
                if e >= 1:
                    pe.wait_ge(hw_f32, 16 * f + 2 * e)
                pe.matmul(WB[:], sel[:, (K_SEL + e) * P:(K_SEL + e + 1) * P], wT_s[:],
                          start=True, stop=True).then_inc(pe_wb, 1)

            def second(f, e):
                if e == 0:
                    pe.matmul(Y[:], b2_s[:], wT_s[:], start=True, stop=False)
                for h in range(HALVES):
                    pe.wait_ge(hw_lo, 16 * f + 2 * e + h + 1)
                    slot = (e % RINGS) * HALVES + h
                    last = product(Y[:], W2 + 2 * e + h, hw_h[:, slot, :], hw_l[:, slot, :], start=False,
                                   stop=(e == EXPERTS - 1 and h == 1))
                last.then_inc(pe_y, 1)

            def iteration(g, gnn, tail, ffn, more):
                d, f = g - 1, g - 2
                if ffn:
                    pe.wait_ge(xnT_split, f + 1)
                    pe.wait_ge(wT_split, f + 1)
                    hidden(f, 0)
                if gnn:
                    pe.wait_ge(xlT_split, g + 1)
                    product(G0[:], CONV1, xlT_h[:], xlT_l[:]).then_inc(pe_conv1, 1)
                    product(G1[:], SE, xlT_h[:], xlT_l[:]).then_inc(pe_s, 1)
                if ffn:
                    hidden(f, 1)
                if gnn:
                    pe.wait_ge(h1_f32, g + 1)
                    product(G0[:], MSG, xlT_h[:], xlT_l[:]).then_inc(pe_msg, 1)
                    pe.wait_ge(h1_split, g + 1)
                    conv2(0, 2)
                if tail:
                    pe.wait_ge(gru_step, 3 * d + 3)
                    transposes(G2, gr).then_inc(pe_outT, 1)
                if gnn:
                    conv2(2, 4)
                if ffn:
                    hidden(f, 2)
                    second(f, 0)
                if gnn:
                    pe.wait_ge(s_split, g + 1)
                    pe.matmul(G1[:], sel[:, K_U * P:(K_U + 1) * P], s_s[:], start=True, stop=True)
                    if tail:
                        pe.wait_ge(x1_ready, d + 1)
                    pe.matmul(G2[:], sel[:, K_V * P:(K_V + 1) * P], s_s[:], start=True, stop=True).then_inc(pe_uv, 1)
                    pe.wait_ge(msg_f32, g + 1)
                    for t in range(NT):
                        last = pe.transpose(G0[:, t * P:(t + 1) * P], msg_f[:, t * P:(t + 1) * P], ident)
                    last.then_inc(pe_msgT, 1)
                    conv2(4, 8)
                if ffn:
                    hidden(f, 3)
                    second(f, 1)
                if tail:
                    if gnn:
                        pe.wait_ge(msg_split, g + 1)
                    pe.wait_ge(xn_ready, d + 1)
                    transposes(G0, flat(xn)).then_inc(pe_xnT, 1)
                if gnn:
                    pe.wait_ge(uv_split, g + 1)
                    dist(0)
                    dist(1)
                    conv2(8, 12)
                    pe.wait_ge(exp_done, NT * g + 1)
                    dist(2)
                    pe.wait_ge(exp_done, NT * g + 2)
                    dist(3)
                if ffn:
                    hidden(f, 4)
                    second(f, 2)
                if tail:
                    pe.wait_ge(xnT_f32, d + 1)
                    pe.matmul(G0[0:EXPERTS, :], vec[:, V_WR:V_WR + EXPERTS], xnT[:], start=True,
                              stop=True).then_inc(pe_router, 1)
                if gnn:
                    conv2(12, TAPS)
                if ffn:
                    hidden(f, 5)
                    second(f, 3)
                if tail:
                    pe.wait_ge(lgT_f32, d + 1)
                    if gnn:
                        pe.wait_ge(exp_done, NT * g + 3)
                if gnn:
                    for j in range(NT):
                        pe.wait_ge(a_split, NT * g + j + 1)
                        pe.matmul(G0[:], msg_h[:, j, :], a_h[:, j, :], start=(j == 0), stop=False)
                        pe.matmul(G0[:], msg_h[:, j, :], a_l[:, j, :], start=False, stop=False)
                        last = pe.matmul(G0[:], msg_l[:, j, :], a_h[:, j, :], start=False, stop=(j == NT - 1))
                    last.then_inc(pe_nmp, 1)
                if tail:
                    for t in range(NT):
                        last = pe.transpose(G1[:, t * EXPERTS:(t + 1) * EXPERTS],
                                            lgT[0:EXPERTS, t * P:(t + 1) * P], cst[0:EXPERTS, 0:EXPERTS])
                    last.then_inc(pe_lgT, 1)
                if ffn:
                    hidden(f, 6)
                    second(f, 4)
                if gnn:
                    pe.wait_ge(xc_split, g + 1)
                    pe.wait_ge(exp_done, NT * g + 4)
                    product(G2[:], HH, xlT_h[:], xlT_l[:], stop=False)
                    product(G2[:], IH, xc_h[:], xc_l[:], start=False, stop=False)
                    pe.wait_ge(nmp_split, g + 1)
                    product(G2[:], IH + 3, nm_h[:], nm_l[:], start=False).then_inc(pe_r, 1)
                    if tail:
                        pe.wait_ge(rt_step, ROUTER_STEPS * d + 1)
                    product(G1[:], HH + 1, xlT_h[:], xlT_l[:], stop=False)
                    product(G1[:], IH + 1, xc_h[:], xc_l[:], start=False, stop=False)
                    product(G1[:], IH + 4, nm_h[:], nm_l[:], start=False).then_inc(pe_z, 1)
                if ffn:
                    hidden(f, 7)
                    second(f, 5)
                if gnn:
                    product(G0[:], HH + 2, xlT_h[:], xlT_l[:])
                    product(C2[:], IH + 2, xc_h[:], xc_l[:], stop=False)
                    product(C2[:], IH + 5, nm_h[:], nm_l[:], start=False).then_inc(pe_n, 1)
                if tail:
                    pe.wait_ge(rt_step, ROUTER_STEPS * d + ROUTER_STEPS)
                    if gnn:
                        pe.wait_ge(r_tanh, g + 1)
                    transposes(G2, flat(w_tok)).then_inc(pe_wT, 1)
                if more:
                    pe.wait_ge(xl_ready, g + 2)
                    pe.wait_ge(z_tanh, g + 1)
                    transposes(G1, flat(xl)).then_inc(pe_xT, 1)
                if ffn:
                    second(f, 6)
                    second(f, 7)
                    pe.wait_ge(y_copied, f + 1)
                    for t in range(NT):
                        last = pe.transpose(Y[:, t * P:(t + 1) * P], y_s[:, t * P:(t + 1) * P], ident)
                    last.then_inc(pe_yT, 1)

            pe.wait_ge(cst_loaded, 16)
            pe.wait_ge(vec_loaded, 16)
            pe.wait_ge(xl_ready, 1)
            transposes(G1, flat(xl)).then_inc(pe_xT, 1)
            pe.wait_ge(sel_done, 1)
            pe.wait_ge(stacked, 1)
            pe.wait_ge(zeroed, 3)
            pe.wait_ge(w_hi_done, len(CHUNKS))
            pe.wait_ge(w_lo_dve, 2)
            pe.wait_ge(w_lo_pool, len(CHUNKS) - 2)
            run(pe, iteration)

        @block.scalar
        def _(act):
            def gelu(f, e):
                for h in range(HALVES):
                    n = 2 * e + h
                    act.wait_ge(pe_h, 16 * f + n + 1)
                    if n >= SLOTS:
                        act.wait_ge(hw_f32, 16 * f + n - SLOTS + 1)
                    nc.scalar.activation(ge[:, n % SLOTS, :], HB[h][:], ACT.Gelu,
                                         bias=vec[:, V_EB1 + n:V_EB1 + n + 1]).then_inc(gelu_done, 1)

            def hidden_hi(f, e):
                for h in range(HALVES):
                    n = 2 * e + h
                    act.wait_ge(hw_f32, 16 * f + n + 1)
                    if e >= RINGS and h == 0:
                        act.wait_ge(pe_y, EXPERTS * f + e - RINGS + 1)
                    nc.scalar.copy(hw_h[:, (e % RINGS) * HALVES + h, :], hw[:, n % SLOTS, :]).then_inc(hw_hi, 1)

            def iteration(g, gnn, tail, ffn, more):
                d, f = g - 1, g - 2
                if ffn:
                    gelu(f, 0)
                if gnn:
                    act.wait_ge(pe_conv1, g + 1)
                    nc.scalar.activation(h1, G0[:], ACT.Relu, scale=dv[:, D_SC1:D_SC1 + 1],
                                         bias=dv[:, D_BI1:D_BI1 + 1]).then_inc(h1_f32, 1)
                    act.wait_ge(pe_s, g + 1)
                    nc.scalar.activation(s_f[0:64, :], G1[0:64, :], ACT.Identity, bias=vec[0:64, V_SE:V_SE + 1])
                    nc.scalar.activation(s_f[64:P, :], G1[64:P, :], ACT.Square,
                                         bias=vec[64:P, V_SE:V_SE + 1]).then_inc(s_f32, 1)
                if ffn:
                    hidden_hi(f, 0)
                    gelu(f, 1)
                if gnn:
                    act.wait_ge(pe_msg, g + 1)
                    nc.scalar.activation(msg_f, G0[:], ACT.Relu, bias=vec[:, V_BM:V_BM + 1]).then_inc(msg_f32, 1)
                if ffn:
                    hidden_hi(f, 1)
                    gelu(f, 2)
                if gnn:
                    act.wait_ge(pe_uv, g + 1)
                    nc.scalar.copy(u_s[:], G1[:])
                    nc.scalar.copy(v_s[:], G2[:]).then_inc(uv_hi, 1)
                    act.wait_ge(pe_msgT, g + 1)
                    nc.scalar.copy(msg_h[:, :, :].rearrange("p t d -> p (t d)"), G0[:]).then_inc(msg_hi, 1)
                if ffn:
                    hidden_hi(f, 2)
                    gelu(f, 3)
                if tail:
                    act.wait_ge(pe_xnT, d + 1)
                    nc.scalar.activation(xnT[:], G0[:], ACT.Identity, scale=vec[:, V_GAMMA:V_GAMMA + 1],
                                         bias=vec[:, V_BETA:V_BETA + 1]).then_inc(xnT_f32, 1)
                if ffn:
                    hidden_hi(f, 3)
                if gnn:
                    for j in range(NT):
                        act.wait_ge(pe_dist, NT * g + j + 1)
                        nc.scalar.activation(ex[:, j, :], DIST[j][:], ACT.Exp, scale=-1.0).then_inc(exp_done, 1)
                if ffn:
                    gelu(f, 4)
                if tail:
                    act.wait_ge(pe_router, d + 1)
                    nc.scalar.activation(lgT[0:EXPERTS, :], G0[0:EXPERTS, :], ACT.Identity,
                                         bias=vec[0:EXPERTS, V_BR:V_BR + 1]).then_inc(lgT_f32, 1)
                if ffn:
                    hidden_hi(f, 4)
                    gelu(f, 5)
                if gnn:
                    act.wait_ge(xc_pre, g + 1)
                    nc.scalar.activation(xc[:], xc[:], ACT.Relu, bias=dv[:, D_BI2:D_BI2 + 1]).then_inc(xc_f32, 1)
                if ffn:
                    hidden_hi(f, 5)
                if gnn:
                    act.wait_ge(pe_nmp, g + 1)
                    nc.scalar.copy(nm_h[:], G0[:]).then_inc(nmp_hi, 1)
                if ffn:
                    gelu(f, 6)
                if tail:
                    act.wait_ge(rt_step, ROUTER_STEPS * d + ROUTER_GAP)
                    nc.scalar.activation(gap_t[:], gap[:], ACT.Tanh, scale=0.5).then_inc(gap_tanh, 1)
                if ffn:
                    hidden_hi(f, 6)
                if gnn:
                    act.wait_ge(pe_r, g + 1)
                    nc.scalar.activation(tr[:], G2[:], ACT.Tanh, scale=0.5,
                                         bias=dv[:, D_R:D_R + 1]).then_inc(r_tanh, 1)
                    act.wait_ge(pe_z, g + 1)
                    nc.scalar.activation(tz[:], G1[:], ACT.Tanh, scale=0.5,
                                         bias=dv[:, D_Z:D_Z + 1]).then_inc(z_tanh, 1)
                if ffn:
                    gelu(f, 7)
                    hidden_hi(f, 7)
                if tail:
                    act.wait_ge(pe_wT, d + 1)
                    nc.scalar.copy(wT_s[:], G2[:]).then_inc(wT_hi, 1)
                if more:
                    act.wait_ge(pe_xT, g + 2)
                    act.wait_ge(xlT_kept, g + 1)
                    nc.scalar.copy(xlT[:], G1[:]).then_inc(xlT_f32, 1)
                if gnn:
                    act.wait_ge(gate_step, 3 * g + 3)
                    nc.scalar.activation(nn[:], tr[:], ACT.Tanh, bias=vec[:, V_IH + 2:V_IH + 3]).then_inc(n_tanh, 1)
                if ffn:
                    act.wait_ge(pe_y, EXPERTS * f + EXPERTS)
                    nc.scalar.copy(y_s, Y[:]).then_inc(y_copied, 1)

            act.wait_ge(cst_loaded, 16)
            act.wait_ge(sel_loaded, 16)
            nc.scalar.copy(sel[:], w_raw[:, 1, 0:K_BLOCKS * P]).then_inc(sel_done, 1)
            act.wait_ge(pe_xT, 1)
            nc.scalar.copy(xlT[:], G1[:]).then_inc(xlT_f32, 1)
            for i, (a, b) in enumerate(CHUNKS):
                act.wait_ge(w_loaded[i], 16)
                nc.scalar.copy(w_hi[:, a:b], w_raw[:, i % 2, 0:b - a]).then_inc(w_hi_done, 1)
            act.wait_ge(vec_loaded, 16)
            act.wait_ge(dv_step, 5)
            run(act, iteration)

        @block.gpsimd
        def _(pool):
            def iteration(g, gnn, tail, ffn, more):
                d, f = g - 1, g - 2

                def hidden_lo(e):
                    for h in range(HALVES):
                        n = 2 * e + h
                        slot = (e % RINGS) * HALVES + h
                        pool.wait_ge(hw_hi, 16 * f + n + 1)
                        nc.gpsimd.tensor_tensor(hw_l[:, slot, :], hw[:, n % SLOTS, :],
                                                hw_h[:, slot, :].bitcast(F32), ALU.subtract).then_inc(hw_lo, 1)

                if ffn:
                    hidden_lo(0)
                if tail:
                    pool.wait_ge(ln2_step, 3 * d + 3)
                    nc.gpsimd.tensor_tensor(rs[:], ve[:], cst[:, C_HALF:C_HALF + NT], ALU.pow).then_inc(ln2_rstd, 1)
                if ffn:
                    hidden_lo(1)
                    hidden_lo(2)
                if more:
                    pool.wait_ge(ln1_step, 3 * g + 6)
                    nc.gpsimd.tensor_tensor(rs[:], ve[:], cst[:, C_HALF:C_HALF + NT], ALU.pow).then_inc(ln1_rstd, 1)
                if ffn:
                    hidden_lo(3)
                if gnn:
                    for j in range(NT):
                        pool.wait_ge(a_hi, NT * g + j + 1)
                        nc.gpsimd.tensor_tensor(a_l[:, j, :], ex[:, j, :], a_h[:, j, :].bitcast(F32),
                                                ALU.subtract).then_inc(a_split, 1)
                if ffn:
                    hidden_lo(4)
                if gnn:
                    pool.wait_ge(xc_hi, g + 1)
                    nc.gpsimd.tensor_tensor(xc_l[:], xc[:], xc_h[:].bitcast(F32), ALU.subtract).then_inc(xc_split, 1)
                if ffn:
                    for e in (5, 6, 7):
                        hidden_lo(e)

            for tile in (h1_h, h1_l):
                nc.gpsimd.memset(tile[:, 0:PAD].bitcast(F32), 0.0)
                nc.gpsimd.memset(tile[:, PAD + NODES:].bitcast(F32), 0.0).then_inc(zeroed, 1)
            nc.gpsimd.memset(w_tok[:], 0.0).then_inc(zeroed, 1)
            pool.wait_ge(cst_loaded, 16)
            pool.wait_ge(dv_step, 1)
            nc.gpsimd.tensor_tensor(dv[:, 6:8], dv[:, 6:8], cst[:, C_HALF:C_HALF + 2], ALU.pow).then_inc(dv_pow, 1)
            pool.wait_ge(ln1_step, 3)
            nc.gpsimd.tensor_tensor(rs[:], ve[:], cst[:, C_HALF:C_HALF + NT], ALU.pow).then_inc(ln1_rstd, 1)
            for i in range(2, len(CHUNKS)):
                a, b = CHUNKS[i]
                pool.wait_ge(w_hi_done, i + 1)
                nc.gpsimd.tensor_tensor(w_lo[:, a:b], w_raw[:, i % 2, 0:b - a], w_hi[:, a:b].bitcast(F32),
                                        ALU.subtract).then_inc(w_lo_pool, 1)
            run(pool, iteration)

        @block.vector
        def _(dve):
            def v2(tile):
                return tile[:, :, :].rearrange("p t d -> p (t d)")

            def split(src, dst_h, dst_l, hi_done, lo_done, g):
                nc.vector.tensor_copy(dst_h, src).then_inc(hi_done, 1)
                dve.wait_ge(hi_done, g + 1)
                nc.vector.tensor_tensor(dst_l, src, dst_h.bitcast(F32), ALU.subtract).then_inc(lo_done, 1)

            def stack(tile, src, pattern):
                return nc.vector.scalar_tensor_tensor(out=tile[:], in0=tile[:].bitcast(F32),
                                                      scalar=cst[:, pattern:pattern + 1], in1=src,
                                                      op0=ALU.mult, op1=ALU.add)

            def carry_wait():
                nc.vector.memset(spare[:], 0.0)

            def statistics(src, step, g, scale, bias):
                for t in range(NT):
                    last = nc.vector.bn_stats(st[:, t, :], src[:, t, :])
                last.then_inc(step, 1)
                dve.wait_ge(step, 3 * g + 1)
                carry_wait()
                for t in range(NT):
                    last = nc.vector.bn_aggr(mv[:, t, :], st[:, t, :])
                last.then_inc(step, 1)
                dve.wait_ge(step, 3 * g + 2)
                nc.vector.tensor_scalar(ve[:], mv[:, :, 1], scale, bias, ALU.mult, ALU.add).then_inc(step, 1)

            def normalize(dst, src, rstd_done, ready, g):
                dve.wait_ge(rstd_done, g + 1)
                for t in range(NT):
                    last = nc.vector.tensor_scalar(dst[:, t, :], src[:, t, :], mv[:, t, 0:1], rs[:, t:t + 1],
                                                   ALU.subtract, ALU.mult)
                last.then_inc(ready, 1)

            def router_steps(d):
                done = [0]

                def step(instruction):
                    done[0] += 1
                    instruction.then_inc(rt_step, 1)
                    dve.wait_ge(rt_step, ROUTER_STEPS * d + done[0])

                def choose():
                    dve.wait_ge(pe_lgT, d + 1)
                    step(nc.vector.tensor_copy(v2(lg), G1[:, 0:NT * EXPERTS]))
                    carry_wait()
                    for t in range(NT):
                        last = nc.vector.max(top[:, t, :], lg[:, t, :])
                    step(last)
                    nc.vector.tensor_tensor(gap[:], top[:, :, 0], top[:, :, 1], ALU.subtract).then_inc(rt_step, 1)
                    done[0] += 1
                    assert done[0] == ROUTER_GAP
                    for t in range(NT):
                        last = nc.vector.max_index(top_i[:, t, :], top[:, t, :], lg[:, t, :])
                    step(last)
                    step(nc.vector.tensor_copy(pick[:], top_i[:, :, 0:2]))

                def weights_of():
                    iota = cst[:, C_IOTA:C_IOTA + EXPERTS].unsqueeze(1).broadcast_to([P, NT * 2, EXPERTS])
                    hots = hot[:, :, :, :].rearrange("p t k e -> p (t k) e")
                    picks = pick[:, :, :].rearrange("p t k -> p (t k)").unsqueeze(2)
                    nc.vector.tensor_tensor(hots, iota, picks.broadcast_to([P, NT * 2, EXPERTS]), ALU.is_equal)
                    dve.wait_ge(gap_tanh, d + 1)
                    nc.vector.tensor_scalar(w12[:, :, 0], gap_t[:], 0.5, 0.5, ALU.mult, ALU.add)
                    step(nc.vector.tensor_scalar(w12[:, :, 1], gap_t[:], -0.5, 0.5, ALU.mult, ALU.add))
                    w12s = w12[:, :, :].rearrange("p t k -> p (t k)").unsqueeze(2)
                    step(nc.vector.tensor_tensor(hots, hots, w12s.broadcast_to([P, NT * 2, EXPERTS]), ALU.mult))
                    for r in range(4):
                        last = nc.vector.tensor_tensor(w_tok[:, :, 32 * r:32 * r + EXPERTS], hot[:, :, 0, :],
                                                       hot[:, :, 1, :], ALU.add)
                    step(last)
                    assert done[0] == ROUTER_STEPS

                return choose, weights_of

            def weigh(f, e):
                for h in range(HALVES):
                    n = 2 * e + h
                    dve.wait_ge(gelu_done, 16 * f + n + 1)
                    if h == 0:
                        dve.wait_ge(pe_wb, EXPERTS * f + e + 1)
                    if n >= SLOTS:
                        dve.wait_ge(hw_lo, 16 * f + n - SLOTS + 1)
                    nc.vector.tensor_tensor(hw[:, n % SLOTS, :], ge[:, n % SLOTS, :], WB[:],
                                            ALU.mult).then_inc(hw_f32, 1)

            def iteration(g, gnn, tail, ffn, more):
                d, f = g - 1, g - 2
                if tail:
                    choose, weights_of = router_steps(d)
                if ffn:
                    weigh(f, 0)
                if gnn:
                    dve.wait_ge(h1_f32, g + 1)
                    split(h1, h1_h[:, PAD:PAD + NODES], h1_l[:, PAD:PAD + NODES], h1_hi, h1_split, g)
                    dve.wait_ge(s_f32, g + 1)
                    nc.vector.tensor_copy(s_s[:], s_f).then_inc(s_hi, 1)
                    dve.wait_ge(s_hi, g + 1)
                    stack(s_s, s_f, C_GV).then_inc(s_split, 1)
                if ffn:
                    weigh(f, 1)
                if tail:
                    if ffn:
                        nc.vector.tensor_copy(x1_keep[:], x1[:]).then_inc(x1_kept, 1)
                    dve.wait_ge(pe_outT, d + 1)
                    dve.wait_ge(x_res_loaded, 16 * d + 16)
                    if ffn:
                        dve.wait_ge(x1_kept, f + 1)
                    nc.vector.tensor_tensor(v2(x1), v2(x_res), G2[:], ALU.add).then_inc(x1_ready, 1)
                    dve.wait_ge(x1_ready, d + 1)
                    statistics(x1, ln2_step, d, 1.0 + EPS, EPS * EPS)
                if gnn:
                    nc.vector.tensor_copy(xlT_keep[:], xlT[:]).then_inc(xlT_kept, 1)
                if ffn:
                    weigh(f, 2)
                if tail:
                    normalize(xn, x1, ln2_rstd, xn_ready, d)
                if gnn:
                    dve.wait_ge(uv_hi, g + 1)
                    stack(u_s, G1[:], C_GU)
                    stack(v_s, G2[:], C_GV).then_inc(uv_split, 1)
                    dve.wait_ge(msg_hi, g + 1)
                    nc.vector.tensor_tensor(v2(msg_l), G0[:], v2(msg_h).bitcast(F32),
                                            ALU.subtract).then_inc(msg_split, 1)
                if ffn:
                    weigh(f, 3)
                if more:
                    dve.wait_ge(x_ln_loaded, 16 * g + 32)
                    statistics(x_ln, ln1_step, g + 1, 1.0, EPS)
                if gnn:
                    dve.wait_ge(adj_loaded, 16 * g + 16)
                    for j in range(NT):
                        dve.wait_ge(exp_done, NT * g + j + 1)
                        nc.vector.tensor_tensor(ex[:, j, :], ex[:, j, :], adj[:, j, :], ALU.mult).then_inc(a_prod, 1)
                        dve.wait_ge(a_prod, NT * g + j + 1)
                        nc.vector.tensor_copy(a_h[:, j, :], ex[:, j, :]).then_inc(a_hi, 1)
                        if j == 1 and more:
                            normalize(xl, x_ln, ln1_rstd, xl_ready, g + 1)
                if ffn:
                    weigh(f, 4)
                if gnn:
                    dve.wait_ge(pe_conv2, g + 1)
                    nc.vector.scalar_tensor_tensor(out=xc[:], in0=C2[:], scalar=dv[:, D_SC2:D_SC2 + 1], in1=xlT[:],
                                                   op0=ALU.mult, op1=ALU.add).then_inc(xc_pre, 1)
                if ffn:
                    weigh(f, 5)
                if gnn:
                    dve.wait_ge(xc_f32, g + 1)
                    nc.vector.tensor_copy(xc_h[:], xc[:]).then_inc(xc_hi, 1)
                if tail:
                    choose()
                if gnn:
                    dve.wait_ge(nmp_hi, g + 1)
                    nc.vector.tensor_tensor(nm_l[:], G0[:], nm_h[:].bitcast(F32), ALU.subtract).then_inc(nmp_split, 1)
                if ffn:
                    weigh(f, 6)
                if tail:
                    weights_of()
                if gnn:
                    dve.wait_ge(r_tanh, g + 1)
                    nc.vector.tensor_scalar(tr[:], tr[:], 0.5, 0.5, ALU.mult, ALU.add).then_inc(gate_step, 1)
                if ffn:
                    weigh(f, 7)
                if tail:
                    if ffn:
                        dve.wait_ge(pe_h, 16 * f + 16)
                    split(xnT[:], xnT_h[:], xnT_l[:], xnT_hi, xnT_split, d)
                if gnn:
                    dve.wait_ge(pe_n, g + 1)
                    dve.wait_ge(gate_step, 3 * g + 1)
                    nc.vector.scalar_tensor_tensor(out=tr[:], in0=G0[:], scalar=vec[:, V_HH + 2:V_HH + 3], in1=tr[:],
                                                   op0=ALU.add, op1=ALU.mult).then_inc(gate_step, 1)
                    dve.wait_ge(gate_step, 3 * g + 2)
                    nc.vector.tensor_tensor(tr[:], tr[:], C2[:], ALU.add).then_inc(gate_step, 1)
                if tail:
                    dve.wait_ge(wT_hi, d + 1)
                    stack(wT_s, G2[:], C_GV).then_inc(wT_split, 1)
                if more:
                    dve.wait_ge(xlT_f32, g + 2)
                    split(xlT[:], xlT_h[:], xlT_l[:], xlT_hi, xlT_split, g + 1)
                if gnn:
                    dve.wait_ge(n_tanh, g + 1)
                    nc.vector.tensor_tensor(gr[:], xlT_keep[:], nn[:], ALU.subtract).then_inc(gru_step, 1)
                    dve.wait_ge(z_tanh, g + 1)
                    dve.wait_ge(gru_step, 3 * g + 1)
                    nc.vector.scalar_tensor_tensor(out=gr[:], in0=tz[:], scalar=1.0, in1=gr[:], op0=ALU.add,
                                                   op1=ALU.mult).then_inc(gru_step, 1)
                    dve.wait_ge(gru_step, 3 * g + 2)
                    nc.vector.scalar_tensor_tensor(out=gr[:], in0=gr[:], scalar=0.5, in1=nn[:], op0=ALU.mult,
                                                   op1=ALU.add).then_inc(gru_step, 1)
                if ffn:
                    dve.wait_ge(pe_yT, f + 1)
                    kept = x1_keep if tail else x1
                    if not gnn:
                        dve.wait_ge(out_stored, 16 * f)
                    nc.vector.tensor_tensor(v2(o_s), v2(kept), Y[:], ALU.add).then_inc(final_done, 1)

            dve.wait_ge(vec_loaded, 16)
            nc.vector.tensor_scalar(dv[:, 6:8], vec[:, V_V1:V_V2 + 1], EPS, None, ALU.add).then_inc(dv_step, 1)
            nc.vector.tensor_tensor(dv[:, D_R:D_Z + 1], vec[:, V_IH:V_IH + 2], vec[:, V_HH:V_HH + 2],
                                    ALU.add).then_inc(dv_step, 1)
            dve.wait_ge(dv_step, 2)
            nc.vector.tensor_scalar(dv[:, D_R:D_Z + 1], dv[:, D_R:D_Z + 1], 0.5, None, ALU.mult)
            dve.wait_ge(dv_pow, 1)
            nc.vector.tensor_tensor(dv[:, D_SC1:D_SC2 + 1], vec[:, V_G1:V_G2 + 1], dv[:, 6:8],
                                    ALU.mult).then_inc(dv_step, 1)
            dve.wait_ge(dv_step, 3)
            nc.vector.tensor_tensor(dv[:, D_BI1:D_BI2 + 1], vec[:, V_M1:V_M2 + 1], dv[:, D_SC1:D_SC2 + 1],
                                    ALU.mult).then_inc(dv_step, 1)
            dve.wait_ge(dv_step, 4)
            nc.vector.tensor_tensor(dv[:, D_BI1:D_BI2 + 1], vec[:, V_B1:V_B2 + 1], dv[:, D_BI1:D_BI2 + 1],
                                    ALU.subtract).then_inc(dv_step, 1)
            dve.wait_ge(cst_loaded, 16)
            dve.wait_ge(x_ln_loaded, 16)
            statistics(x_ln, ln1_step, 0, 1.0, EPS)
            normalize(xl, x_ln, ln1_rstd, xl_ready, 0)
            dve.wait_ge(sel_done, 1)
            cols = slice(K_B2 * P, (K_B2 + 1) * P)
            nc.vector.scalar_tensor_tensor(out=b2_s[:], in0=sel[:, cols].bitcast(F32), scalar=cst[:, C_GU:C_GU + 1],
                                           in1=w_raw[:, 1, cols], op0=ALU.mult, op1=ALU.add).then_inc(stacked, 1)
            dve.wait_ge(xlT_f32, 1)
            split(xlT[:], xlT_h[:], xlT_l[:], xlT_hi, xlT_split, 0)
            for i in range(2):
                a, b = CHUNKS[i]
                dve.wait_ge(w_hi_done, i + 1)
                nc.vector.tensor_tensor(w_lo[:, a:b], w_raw[:, i, 0:b - a], w_hi[:, a:b].bitcast(F32),
                                        ALU.subtract).then_inc(w_lo_dve, 1)
            run(dve, iteration)


ROUTER_GAP = 3
ROUTER_STEPS = 8


def kernel(**inputs):
    import concourse.bacc as bacc
    from concourse.bass_utils import run_bass_kernel_spmd

    a = {k: np.asarray(v) for k, v in inputs.items()}
    g = {k.removeprefix("L0_gnn_"): v for k, v in a.items()}
    e = {k.removeprefix("L0_ffn_"): v for k, v in a.items()}

    w = np.zeros((P, WCOLS), np.float32)
    k = selections()

    def put(block, value):
        w[:value.shape[0], block * P:block * P + value.shape[1]] = value

    for r in range(4):
        w[:, SE * P + 32 * r:SE * P + 32 * r + 3] = g["w_se"].T
        k[32 * r:32 * r + EXPERTS, K_B2] = e["b2"]
    put(CONV1, g["conv1_w"][:, :, 0].T)
    put(MSG, g["w_msg"].T)
    for tap in range(TAPS):
        put(CONV2 + tap, g["conv2_w"][:, :, tap].T)
    for gate in range(3):
        rows = slice(gate * P, (gate + 1) * P)
        put(IH + gate, g["w_ih"][rows, 0:P].T)
        put(IH + 3 + gate, g["w_ih"][rows, P:2 * P].T)
        put(HH + gate, g["w_hh"][rows].T)
    for n in range(EXPERTS):
        for h in range(HALVES):
            half = slice(h * P, (h + 1) * P)
            put(W1 + 2 * n + h, e["W1"][n][:, half])
            put(W2 + 2 * n + h, e["W2"][n][half, :])

    v = np.zeros((P, VCOLS), np.float32)
    for col, name in ((V_G1, "bn1_g"), (V_G2, "bn2_g"), (V_V1, "bn1_v"), (V_V2, "bn2_v"), (V_B1, "bn1_b"),
                      (V_B2, "bn2_b"), (V_M1, "bn1_m"), (V_M2, "bn2_m")):
        v[:, col] = g[name]
    for gate in range(3):
        v[:, V_IH + gate] = g["b_ih"][gate * P:(gate + 1) * P]
        v[:, V_HH + gate] = g["b_hh"][gate * P:(gate + 1) * P]
    v[:, V_GAMMA] = e["gamma"]
    v[:, V_BETA] = e["beta"]
    for r in range(4):
        v[32 * r:32 * r + 3, V_SE] = g["b_se"]
        v[32 * r + 3, V_SE] = 1.0
    for n in range(EXPERTS):
        for h in range(HALVES):
            v[:, V_EB1 + 2 * n + h] = e["b1"][n, h * P:(h + 1) * P]
    v[:EXPERTS, V_BR] = e["br"]
    v[:, V_BM] = g["b_msg"]
    v[:, V_WR:V_WR + EXPERTS] = e["Wr"]

    arrays = {
        "x": np.ascontiguousarray(a["x"]),
        "adj_t": np.ascontiguousarray(a["adj"].transpose(0, 2, 1)),
        "weights": w,
        "stacks": k.reshape(P, K_BLOCKS * P),
        "vectors": v,
        "consts": constants(),
    }
    nc = bacc.Bacc("TRN2", target_bir_lowering=False, num_devices=1)
    args = [nc.dram_tensor(n, t.shape, F32, kind="ExternalInput").ap() for n, t in arrays.items()]
    out = nc.dram_tensor("out", a["x"].shape, F32, kind="ExternalOutput").ap()
    gnn_moe(nc, *args, out)
    result = run_bass_kernel_spmd(nc, [arrays], core_ids=[0])
    return result.results[0]["out"]
```

```python
from contextlib import ExitStack

import numpy as np

import concourse.bass as bass
from concourse import mybir

F32 = mybir.dt.float32
F32R = mybir.dt.float32r
U32 = mybir.dt.uint32
ALU = mybir.AluOpType
ACT = mybir.ActivationFunctionType

P = 128
GRAPHS = 16
NODES = 512
NT = NODES // P
TAPS = 17
PAD = TAPS // 2
SPACE = 3
S_ROWS = [0, SPACE, 2 * SPACE, 3 * SPACE, 64, 64 + SPACE, 96, 96 + SPACE]
EXPERTS = 8
HALVES = 2
EPS = 1e-5
LAG = 2
SLOTS = 4
RINGS = 4

SE, CONV1, MSG = 0, 1, 2
CONV_A = 3
TAPS_A = (TAPS + 1) // 2
CONV_B = CONV_A + TAPS_A
TAPS_B = TAPS // 2
IH = CONV_B + TAPS_B
HH = IH + 6
W1 = HH + 3
W2 = W1 + 16
BLOCKS = W2 + 16
CONV_S = BLOCKS
WCOLS = BLOCKS * P
HALF = NODES // 2
PADDED = NODES + 2 * PAD

(V_G1, V_G2, V_V1, V_V2, V_B1, V_B2, V_M1, V_M2, V_IH, V_HH, V_GAMMA, V_BETA, V_SE, V_EB1, V_BR, V_BM,
 V_WR) = (0, 1, 2, 3, 4, 5, 6, 7, 8, 11, 14, 15, 16, 17, 33, 33 + EXPERTS, 34 + EXPERTS)
VCOLS = V_WR + EXPERTS
D_SC1, D_SC2, D_BI1, D_BI2, D_R, D_Z = range(6)

C_ID = 0
C_GU = C_ID + P
C_GV = C_GU + 1
C_DU = C_GV + 1
C_DV = C_DU + 1
C_IOTA = C_DV + 1
C_HALF = C_IOTA + EXPERTS
CCOLS = C_HALF + NT


def constants():
    c = np.zeros((P, CCOLS), np.float32)
    c[:, C_ID:C_ID + P] = np.eye(P)
    for r in range(4):
        c[32 * r:32 * r + 32, C_GU] = 0.0 if r < 2 else -1.0
        c[32 * r:32 * r + 32, C_GV] = 0.0 if r % 2 == 0 else -1.0
    for i in range(SPACE):
        c[[2 * SPACE + i, 3 * SPACE + i], C_DU] = -1.0
        c[[SPACE + i, 3 * SPACE + i], C_DV] = -1.0
        c[2 * 32 + SPACE + i, C_DU] = -1.0
        c[3 * 32 + SPACE + i, C_DV] = -1.0
    c[:, C_IOTA:C_IOTA + EXPERTS] = np.arange(EXPERTS)
    c[:, C_HALF:C_HALF + NT] = -0.5
    return c


def gnn_moe(nc, x, adj_t, weights, b2_rows, vectors, consts, w_rows, out):
    x_v = x.rearrange("g (t p) d -> g p t d", p=P)
    adj_v = adj_t.rearrange("g (t p) n -> g p t n", p=P)
    out_v = out.rearrange("g (t p) d -> g p t d", p=P)

    with ExitStack() as ctx:
        def sb(name, shape, dt=F32):
            return ctx.enter_context(nc.sbuf_tensor(name, shape, dt))

        def under(name, shape, dt=F32):
            with nc.sbuf_tensor(name, shape, dt) as tensor:
                return tensor

        def bank(name):
            return ctx.enter_context(nc.psum_tensor(name, [P, 512], F32))

        def sem(name):
            return ctx.enter_context(nc.semaphore(name))

        w_raw = sb("w_raw", [P, 2 * SLOTS * NODES])
        w_hi = sb("w_hi", [P, WCOLS + TAPS_B * P], F32R)
        w_lo = sb("w_lo", [P, WCOLS + TAPS_B * P], F32R)
        vec = sb("vec", [P, VCOLS])
        dv = sb("dv", [P, 8])
        cst = sb("cst", [P, CCOLS])
        b2_s = sb("b2_s", [P, P], F32R)
        ge = w_raw[:, 0:SLOTS * NODES].rearrange("p (s n) -> p s n", s=SLOTS)
        hw = w_raw[:, SLOTS * NODES:].rearrange("p (s n) -> p s n", s=SLOTS)
        x_ln = sb("x_ln", [P, NT, P])
        x_res = sb("x_res", [P, NT, P])
        adj = sb("adj", [P, NT, NODES])
        st = sb("st", [P, NT, 6])
        mv = sb("mv", [P, NT, 2])
        ve = sb("ve", [P, NT])
        spare = sb("spare", [P, 2])
        rs = sb("rs", [P, NT])
        xl = sb("xl", [P, NT, P])
        xlT = sb("xlT", [P, NODES])
        xlT_keep = sb("xlT_keep", [P, NODES])
        xlT_h = sb("xlT_h", [P, NODES], F32R)
        xlT_l = sb("xlT_l", [P, NODES], F32R)
        h1 = sb("h1", [P, PADDED + 2])
        diff = sb("diff", [P, 2, PADDED // 2])
        cv_h = sb("cv_h", [P, 3, PADDED // 2], F32R)
        cv_l = sb("cv_l", [P, 3, PADDED // 2], F32R)
        u_s = sb("u_s", [P, NODES], F32R)
        v_s = sb("v_s", [P, NODES], F32R)
        msg_h = sb("msg_h", [P, NT, P], F32R)
        msg_l = sb("msg_l", [P, NT, P], F32R)
        a_l = under("a_l", [P, NT, NODES], F32R)
        ex = sb("ex", [P, NT, NODES])
        s_f, msg_f, y_s = (ex[:, j, :] for j in range(1, NT))
        a_h = sb("a_h", [P, NT, NODES], F32R)
        xc_h = sb("xc_h", [P, NODES], F32R)
        xc_l = sb("xc_l", [P, NODES], F32R)
        nm_h, nm_l = (tile[:, :, :].rearrange("p h m -> p (h m)")[:, 0:NODES] for tile in (cv_h, cv_l))
        tr = sb("tr", [P, NODES])
        tz = sb("tz", [P, NODES])
        both = tz[:, 0:HALF]
        gr = sb("gr", [P, NODES])
        nn = sb("nn", [P, NODES])
        xc = nn
        x1 = sb("x1", [P, NT, P])
        x1_keep = sb("x1_keep", [P, NT, P])
        xnT = sb("xnT", [P, NODES])
        xnT_h = sb("xnT_h", [P, NODES], F32R)
        xnT_l = sb("xnT_l", [P, NODES], F32R)
        wT = diff[:, :, :].rearrange("p h m -> p (h m)")[0:EXPERTS, 0:NODES]
        wb = sb("wb", [P, 2, NODES])
        lg = sb("lg", [P, NT, EXPERTS])
        top = sb("top", [P, NT, 8])
        top_i = sb("top_i", [P, NT, 8], U32)
        pick = sb("pick", [P, NT, 2])
        gap = sb("gap", [P, NT])
        gap_t = sb("gap_t", [P, NT])
        w12 = sb("w12", [P, NT, 2])
        hot = sb("hot", [P, NT, 2, EXPERTS])
        w_tok = sb("w_tok", [P, NT, P])
        wT_s = sb("wT_s", [P, NODES], F32R)
        stage = under("stage", [P, (10 + 16) * P])
        hw_h = sb("hw_h", [P, RINGS * HALVES, NODES], F32R)
        hw_l = sb("hw_l", [P, RINGS * HALVES, NODES], F32R)
        o_s = sb("o_s", [P, NT, P])
        xn = o_s
        parts = {
            "first": (SE, 3, w_raw[:, (TAPS + TAPS_B) * P:(TAPS + TAPS_B + 3) * P]),
            "conv_s": (CONV_S, TAPS_B, w_raw[:, TAPS * P:(TAPS + TAPS_B) * P]),
            "conv_a": (CONV_A, TAPS_A, w_raw[:, 0:TAPS_A * P]),
            "conv_b": (CONV_B, TAPS_B, w_raw[:, TAPS_A * P:TAPS * P]),
            "gates": (IH, 9, stage[:, 0:9 * P]),
            "w1": (W1, 16, stage[:, 10 * P:]),
            "w2": (W2, 16, w_raw[:, 0:16 * P]),
        }
        b2_raw = stage[:, 9 * P:10 * P]
        G0, G1, G2, H0, H1, Y, C2, M = (bank(n) for n in ("G0", "G1", "G2", "H0", "H1", "Y", "C2", "M"))
        HB = (H0, H1)
        DIST = (G1, G2, G1, G2)

        w_loaded, w_hi_done, w_lo_done = (
            {name: sem(f"{what}_{name}") for name in parts} for what in ("w_loaded", "w_hi", "w_lo"))
        vec_loaded, cst_loaded = sem("vec_loaded"), sem("cst_loaded")
        conv_summed = sem("conv_summed")
        zeroed, rows_set = sem("zeroed"), sem("rows_set")
        stacked = sem("stacked")
        b2_loaded, b2_hi = sem("b2_loaded"), sem("b2_hi")
        dv_step, dv_pow = sem("dv_step"), sem("dv_pow")
        x_ln_loaded, x_res_loaded, adj_loaded, out_stored = map(
            sem, ("x_ln_loaded", "x_res_loaded", "adj_loaded", "out_stored"))
        w_stored = sem("w_stored")
        wb_loaded = [sem(f"wb_loaded{i}") for i in range(2)]
        pe_xnT, pe_xT, pe_conv1, pe_s, pe_msg, pe_router, pe_dist, pe_wT, pe_conv2, pe_msgT = map(
            sem, ("pe_xnT", "pe_xT", "pe_conv1", "pe_s", "pe_msg", "pe_router", "pe_dist", "pe_wT",
                  "pe_conv2", "pe_msgT"))
        pe_conv_s = sem("pe_conv_s")
        pe_h, pe_y, pe_nmp, pe_r, pe_z, pe_n, pe_outT, pe_yT = map(
            sem, ("pe_h", "pe_y", "pe_nmp", "pe_r", "pe_z", "pe_n", "pe_outT", "pe_yT"))
        xnT_f32, xlT_f32, h1_f32, s_f32, msg_f32, msg_hi, gap_tanh, uv_hi, exp_done, wT_hi = map(
            sem, ("xnT_f32", "xlT_f32", "h1_f32", "s_f32", "msg_f32", "msg_hi", "gap_tanh", "uv_hi",
                  "exp_done", "wT_hi"))
        both_f32, wT_f32 = sem("both_f32"), sem("wT_f32")
        gelu_done, hw_hi, xc_hi, nmp_hi, r_tanh, z_tanh, n_tanh, y_copied = map(
            sem, ("gelu_done", "hw_hi", "xc_hi", "nmp_hi", "r_tanh", "z_tanh", "n_tanh", "y_copied"))
        ln1_step, xl_ready, ln2_step, xn_ready, x1_ready, x1_kept = map(
            sem, ("ln1_step", "xl_ready", "ln2_step", "xn_ready", "x1_ready", "x1_kept"))
        xnT_hi, xnT_split, xlT_hi, xlT_split, odd_hi, odd_split, msg_split = map(
            sem, ("xnT_hi", "xnT_split", "xlT_hi", "xlT_split", "odd_hi", "odd_split", "msg_split"))
        xlT_kept, rt_step, uv_split, wT_split, a_prod, a_hi, xc_pre, xc_split, hw_f32 = map(
            sem, ("xlT_kept", "rt_step", "uv_split", "wT_split", "a_prod", "a_hi", "xc_pre", "xc_split", "hw_f32"))
        diff_f32, diff_hi, diff_split = map(sem, ("diff_f32", "diff_hi", "diff_split"))
        nmp_split, gate_step, gru_step, final_done = map(
            sem, ("nmp_split", "gate_step", "gru_step", "final_done"))
        hw_lo_dve = sem("hw_lo_dve")
        ln1_rstd, ln2_rstd, a_split, xc_base, hw_lo = map(
            sem, ("ln1_rstd", "ln2_rstd", "a_split", "xc_base", "hw_lo"))

        def hi(block, width=P):
            return w_hi[:, block * P:block * P + width]

        def lo(block, width=P):
            return w_lo[:, block * P:block * P + width]

        def is_graph(g, n):
            return isinstance(g, int) and g == n

        def wait_split(engine, f, n):
            if not is_graph(f, GRAPHS - 1):
                engine.wait_ge(hw_lo, 16 * f + n + 1)
            elif n % 2:
                engine.wait_ge(hw_lo_dve, n // 2 + 1)
            else:
                engine.wait_ge(hw_lo, 16 * f + n // 2 + 1)

        def hidden_bank(e, h, gnn):
            return (G1, C2)[h] if not gnn and e >= 2 and e % 2 == 0 else HB[h]

        def run(engine, iteration):
            iteration(0, True, False, False, True)
            iteration(1, True, True, False, True)
            iteration(2, True, True, True, True)
            with engine.Fori(3, GRAPHS - 1) as g:
                iteration(g, True, True, True, True)
            iteration(GRAPHS - 1, True, True, True, False)
            iteration(GRAPHS, False, True, True, False)
            iteration(GRAPHS + 1, False, False, True, False)

        block = ctx.enter_context(nc.Block())

        @block.sync
        def _(sp):
            def load(name):
                first, blocks, raw = parts[name]
                sp.dma_start(raw, weights[:, first * P:(first + blocks) * P]).then_inc(w_loaded[name], 16)

            sp.dma_start(x_ln[:], x_v[0]).then_inc(x_ln_loaded, 16)
            sp.dma_start(vec[:], vectors).then_inc(vec_loaded, 16)
            sp.dma_start(cst[:], consts).then_inc(cst_loaded, 16)
            for name in ("first", "conv_a", "conv_b"):
                load(name)
            sp.dma_start(b2_raw, b2_rows).then_inc(b2_loaded, 16)
            sp.dma_start(adj[:], adj_v[0]).then_inc(adj_loaded, 16)
            load("gates")
            load("w1")
            sp.wait_ge(w_lo_done["conv_a"], 1)
            sp.wait_ge(w_lo_done["conv_b"], 1)
            load("w2")

            def broadcast(f, e):
                sp.wait_ge(hw_f32, 16 * f + 2 * (e - 2) + 2)
                sp.dma_start(wb[:, e % 2, :], w_rows[e:e + 1, :].broadcast_to([P, NODES])).then_inc(wb_loaded[e % 2], 16)

            def iteration(g, gnn, tail, ffn, more):
                d, f = g - 1, g - 2
                if more:
                    sp.wait_ge(xl_ready, g + 1)
                    sp.dma_start(x_ln[:], x_v[g + 1]).then_inc(x_ln_loaded, 16)
                if ffn:
                    broadcast(f, 2)
                    broadcast(f, 3)
                if gnn:
                    if tail:
                        sp.wait_ge(x1_ready, d + 1)
                    sp.dma_start(x_res[:], x_v[g]).then_inc(x_res_loaded, 16)
                if ffn:
                    broadcast(f, 4)
                    broadcast(f, 5)
                if more:
                    sp.wait_ge(a_prod, NT * g + NT)
                    sp.dma_start(adj[:], adj_v[g + 1]).then_inc(adj_loaded, 16)
                if ffn:
                    broadcast(f, 6)
                    broadcast(f, 7)
                if tail:
                    sp.wait_ge(wT_f32, d + 1)
                    sp.dma_start(w_rows, wT).then_inc(w_stored, 16)
                    sp.wait_ge(w_stored, 16 * d + 16)
                    for e in range(2):
                        sp.dma_start(wb[:, e, :], w_rows[e:e + 1, :].broadcast_to([P, NODES])).then_inc(wb_loaded[e], 16)
                if ffn:
                    sp.wait_ge(final_done, f + 1)
                    sp.dma_start(out_v[f], o_s[:]).then_inc(out_stored, 16)

            run(sp, iteration)
            sp.wait_ge(out_stored, 16 * GRAPHS)

        @block.tensor
        def _(pe):
            ident = cst[:, C_ID:C_ID + P]

            def product(psum, w, rhs_h, rhs_l, start=True, stop=True):
                pe.matmul(psum, hi(w), rhs_h, start=start, stop=False)
                pe.matmul(psum, hi(w), rhs_l, start=False, stop=False)
                return pe.matmul(psum, lo(w), rhs_h, start=False, stop=stop)

            def transposes(psum, tile):
                for t in range(NT):
                    last = pe.transpose(psum[:, t * P:(t + 1) * P], tile[:, t * P:(t + 1) * P], ident)
                return last

            def flat(tile):
                return tile[:, :, :].rearrange("p t d -> p (t d)")

            def conv_sum(a, b):
                for i in range(a, b):
                    w = CONV_S + i if i < TAPS_B else CONV_A + i
                    last = product(C2[:, 0:HALF], w, cv_h[:, 2, i:i + HALF], cv_l[:, 2, i:i + HALF],
                                   start=(i == 0), stop=(i == TAPS_A - 1))
                if b == TAPS_A:
                    last.then_inc(pe_conv_s, 1)

            def conv_diff(a, b):
                for k in range(a, b):
                    h, i = divmod(k, TAPS_A)
                    last = product(C2[:, h * HALF:(h + 1) * HALF], CONV_A + k, cv_h[:, h, i:i + HALF],
                                   cv_l[:, h, i:i + HALF], start=(i == 0), stop=(k in (TAPS_A - 1, TAPS - 1)))
                if b == TAPS:
                    last.then_inc(pe_conv2, 1)

            def dist(j):
                pe.matmul(DIST[j][:], u_s[:, j * P:(j + 1) * P], v_s[:], start=True, stop=True).then_inc(pe_dist, 1)

            def hidden(f, e, gnn):
                before = 1 if gnn or e < 2 else 2
                for h in range(HALVES):
                    if e >= before and (gnn or e != 2):
                        pe.wait_ge(gelu_done, 16 * f + 2 * (e - before) + h + 1)
                    product(hidden_bank(e, h, gnn)[:], W1 + 2 * e + h, xnT_h[:], xnT_l[:]).then_inc(pe_h, 1)

            def behind(f, e, gnn):
                lag = LAG if gnn else LAG + 1
                if e >= lag:
                    second(f, e - lag)

            def normalized(d):
                pe.wait_ge(xn_ready, d + 1)
                transposes(G0, flat(xn)).then_inc(pe_xnT, 1)

            def second(f, e):
                if e == 0:
                    pe.wait_ge(wT_split, f + 1)
                    if not is_graph(f, 0):
                        pe.wait_ge(final_done, f)
                    pe.matmul(Y[:], b2_s[:], wT_s[:], start=True, stop=False)
                for h in range(HALVES):
                    wait_split(pe, f, 2 * e + h)
                    slot = (e % RINGS) * HALVES + h
                    last = product(Y[:], W2 + 2 * e + h, hw_h[:, slot, :], hw_l[:, slot, :], start=False,
                                   stop=(e == EXPERTS - 1 and h == 1))
                last.then_inc(pe_y, 1)

            def iteration(g, gnn, tail, ffn, more):
                d, f = g - 1, g - 2
                if gnn:
                    pe.wait_ge(xlT_split, g + 1)
                    product(M[:], CONV1, xlT_h[:], xlT_l[:]).then_inc(pe_conv1, 1)
                    product(G1[:], SE, xlT_h[:], xlT_l[:]).then_inc(pe_s, 1)
                if ffn:
                    hidden(f, 1, gnn)
                if gnn:
                    if tail:
                        pe.wait_ge(gate_step, 3 * d + 2)
                    product(G0[:], MSG, xlT_h[:], xlT_l[:]).then_inc(pe_msg, 1)
                    if is_graph(g, 0):
                        pe.wait_ge(w_lo_done["conv_s"], 1)
                        pe.wait_ge(w_lo_done["conv_a"], 1)
                    pe.wait_ge(odd_split, g + 1)
                    conv_sum(0, 5)
                if tail:
                    pe.wait_ge(gru_step, 3 * d + 3)
                    transposes(G2, gr).then_inc(pe_outT, 1)
                if gnn:
                    conv_sum(5, TAPS_A)
                if ffn:
                    hidden(f, 2, gnn)
                    behind(f, 2, gnn)
                if is_graph(g, 2):
                    pe.wait_ge(stacked, 1)
                if gnn:
                    pe.wait_ge(msg_f32, g + 1)
                    pe.wait_ge(h1_f32, g + 1)
                    for t in range(NT):
                        last = pe.transpose(M[:, t * P:(t + 1) * P], msg_f[:, t * P:(t + 1) * P], ident)
                    last.then_inc(pe_msgT, 1)
                if ffn:
                    hidden(f, 3, gnn)
                if gnn:
                    if is_graph(g, 0):
                        pe.wait_ge(w_lo_done["conv_b"], 1)
                    pe.wait_ge(both_f32, g + 1)
                    pe.wait_ge(diff_split, g + 1)
                    conv_diff(0, 4)
                if ffn:
                    behind(f, 3, gnn)
                if gnn:
                    if is_graph(g, 0):
                        pe.wait_ge(rows_set, 1)
                    pe.wait_ge(uv_split, g + 1)
                    dist(0)
                    if tail:
                        pe.wait_ge(x1_ready, d + 1)
                    dist(1)
                    conv_diff(4, 7)
                if tail and gnn and ffn:
                    normalized(d)
                if gnn:
                    conv_diff(7, 10)
                if ffn:
                    hidden(f, 4, gnn)
                    behind(f, 4, gnn)
                if tail and not gnn:
                    normalized(d)
                if gnn:
                    pe.wait_ge(exp_done, NT * g + 1)
                    dist(2)
                    pe.wait_ge(exp_done, NT * g + 2)
                    dist(3)
                if gnn:
                    conv_diff(10, TAPS)
                if ffn:
                    behind(f, 5, gnn)
                    hidden(f, 5, gnn)
                if tail and not ffn:
                    normalized(d)
                if gnn:
                    if is_graph(g, 0):
                        pe.wait_ge(w_lo_done["gates"], 1)
                    pe.wait_ge(exp_done, NT * g + 3)
                    product(G1[:], HH + 1, xlT_h[:], xlT_l[:], stop=False)
                    pe.wait_ge(exp_done, NT * g + 4)
                    product(G2[:], HH, xlT_h[:], xlT_l[:], stop=False)
                if tail:
                    pe.wait_ge(xnT_f32, d + 1)
                if gnn:
                    for j in range(NT):
                        pe.wait_ge(a_split, NT * g + j + 1)
                        pe.matmul(G0[:], msg_h[:, j, :], a_h[:, j, :], start=(j == 0), stop=False)
                        pe.matmul(G0[:], msg_h[:, j, :], a_l[:, j, :], start=False, stop=False)
                        last = pe.matmul(G0[:], msg_l[:, j, :], a_h[:, j, :], start=False, stop=(j == NT - 1))
                    last.then_inc(pe_nmp, 1)
                if tail:
                    if gnn:
                        pe.wait_ge(msg_split, g + 1)
                    for t in range(NT):
                        last = pe.matmul(M[:, t * EXPERTS:(t + 1) * EXPERTS], xnT[:, t * P:(t + 1) * P],
                                         vec[:, V_WR:V_WR + EXPERTS], start=True, stop=True)
                    last.then_inc(pe_router, 1)
                if ffn:
                    hidden(f, 6, gnn)
                    behind(f, 6, gnn)
                if gnn:
                    pe.wait_ge(xc_split, g + 1)
                    product(G2[:], IH, xc_h[:], xc_l[:], start=False, stop=False)
                    pe.wait_ge(nmp_split, g + 1)
                    product(G2[:], IH + 3, nm_h, nm_l, start=False).then_inc(pe_r, 1)
                    product(G1[:], IH + 1, xc_h[:], xc_l[:], start=False, stop=False)
                    product(G1[:], IH + 4, nm_h, nm_l, start=False).then_inc(pe_z, 1)
                if ffn:
                    hidden(f, 7, gnn)
                    behind(f, 7, gnn)
                if tail:
                    pe.wait_ge(rt_step, ROUTER_STEPS * d + ROUTER_STEPS)
                    if gnn:
                        pe.wait_ge(r_tanh, g + 1)
                    if is_graph(d, 0):
                        pe.wait_ge(zeroed, 2)
                    transposes(G2, flat(w_tok)).then_inc(pe_wT, 1)
                if gnn:
                    product(G0[:], HH + 2, xlT_h[:], xlT_l[:])
                if more:
                    pe.wait_ge(xl_ready, g + 2)
                    if tail:
                        pe.wait_ge(rt_step, ROUTER_STEPS * d + 1)
                    else:
                        pe.wait_ge(msg_split, g + 1)
                    transposes(M, flat(xl)).then_inc(pe_xT, 1)
                if gnn:
                    product(C2[:], IH + 2, xc_h[:], xc_l[:], stop=False)
                    product(C2[:], IH + 5, nm_h, nm_l, start=False).then_inc(pe_n, 1)
                if is_graph(g, 1):
                    pe.wait_ge(w_lo_done["w1"], 1)
                    pe.wait_ge(w_lo_done["w2"], 1)
                if ffn:
                    if not gnn:
                        second(f, 5)
                    second(f, 6)
                    second(f, 7)
                if tail:
                    pe.wait_ge(xnT_split, d + 1)
                    hidden(d, 0, gnn)
                if ffn:
                    pe.wait_ge(y_copied, f + 1)
                    for t in range(NT):
                        last = pe.transpose(Y[:, t * P:(t + 1) * P], y_s[:, t * P:(t + 1) * P], ident)
                    last.then_inc(pe_yT, 1)

            pe.wait_ge(cst_loaded, 16)
            pe.wait_ge(vec_loaded, 16)
            pe.wait_ge(xl_ready, 1)
            transposes(M, flat(xl)).then_inc(pe_xT, 1)
            pe.wait_ge(w_lo_done["first"], 1)
            run(pe, iteration)

        @block.scalar
        def _(act):
            def operands_hi(g):
                act.wait_ge(s_f32, g + 1)
                nc.scalar.copy(u_s[0:96, :], s_f[0:96, :])
                nc.scalar.copy(v_s[0:64, :], s_f[0:64, :])
                nc.scalar.copy(v_s[96:P, :], s_f[96:P, :]).then_inc(uv_hi, 1)

            def w_hi_part(name):
                first, blocks, raw = parts[name]
                if name == "conv_s":
                    act.wait_ge(conv_summed, 1)
                else:
                    act.wait_ge(w_loaded[name], 16)
                nc.scalar.copy(w_hi[:, first * P:(first + blocks) * P], raw).then_inc(w_hi_done[name], 1)

            def gelu(f, e, gnn):
                for h in range(HALVES):
                    n = 2 * e + h
                    act.wait_ge(pe_h, 16 * f + n + 1)
                    if n >= SLOTS:
                        act.wait_ge(hw_f32, 16 * f + n - SLOTS + 1)
                    nc.scalar.activation(ge[:, n % SLOTS, :], hidden_bank(e, h, gnn)[:], ACT.Gelu,
                                         bias=vec[:, V_EB1 + n:V_EB1 + n + 1]).then_inc(gelu_done, 1)

            def hidden_hi(f, e):
                for h in range(HALVES):
                    n = 2 * e + h
                    act.wait_ge(hw_f32, 16 * f + n + 1)
                    if e >= RINGS and h == 0:
                        act.wait_ge(pe_y, EXPERTS * f + e - RINGS + 1)
                    nc.scalar.copy(hw_h[:, (e % RINGS) * HALVES + h, :], hw[:, n % SLOTS, :]).then_inc(hw_hi, 1)

            def iteration(g, gnn, tail, ffn, more):
                d, f = g - 1, g - 2
                if ffn:
                    gelu(f, 0, gnn)
                if gnn:
                    act.wait_ge(pe_conv1, g + 1)
                    nc.scalar.activation(h1[:, PAD:PAD + NODES], M[:], ACT.Relu, scale=dv[:, D_SC1:D_SC1 + 1],
                                         bias=dv[:, D_BI1:D_BI1 + 1]).then_inc(h1_f32, 1)
                    act.wait_ge(pe_s, g + 1)
                    nc.scalar.activation(s_f[0:64, :], G1[0:64, :], ACT.Identity, bias=vec[0:64, V_SE:V_SE + 1])
                    nc.scalar.activation(s_f[64:P, :], G1[64:P, :], ACT.Square,
                                         bias=vec[64:P, V_SE:V_SE + 1]).then_inc(s_f32, 1)
                if ffn:
                    gelu(f, 1, gnn)
                    hidden_hi(f, 0)
                if gnn:
                    act.wait_ge(pe_msg, g + 1)
                    nc.scalar.activation(msg_f, G0[:], ACT.Relu, bias=vec[:, V_BM:V_BM + 1]).then_inc(msg_f32, 1)
                    if not ffn:
                        operands_hi(g)
                if ffn:
                    hidden_hi(f, 1)
                if gnn:
                    act.wait_ge(pe_conv_s, g + 1)
                    nc.scalar.activation(both, C2[:, 0:HALF], ACT.Identity, scale=dv[:, D_SC2:D_SC2 + 1],
                                         bias=dv[:, D_BI2:D_BI2 + 1]).then_inc(both_f32, 1)
                if ffn:
                    gelu(f, 2, gnn)
                if gnn:
                    if ffn:
                        operands_hi(g)
                    act.wait_ge(pe_msgT, g + 1)
                    nc.scalar.copy(msg_h[:, :, :].rearrange("p t d -> p (t d)"), M[:]).then_inc(msg_hi, 1)
                if ffn:
                    hidden_hi(f, 2)
                    gelu(f, 3, gnn)
                if ffn:
                    hidden_hi(f, 3)
                if gnn:
                    for j in range(NT):
                        act.wait_ge(pe_dist, NT * g + j + 1)
                        nc.scalar.activation(ex[:, j, :], DIST[j][:], ACT.Exp, scale=2.0).then_inc(exp_done, 1)
                if is_graph(g, 0):
                    w_hi_part("w1")
                if is_graph(g, 1):
                    w_hi_part("w2")
                if ffn:
                    gelu(f, 4, gnn)
                if tail:
                    act.wait_ge(pe_xnT, d + 1)
                    nc.scalar.activation(xnT[:], G0[:], ACT.Identity, scale=vec[:, V_GAMMA:V_GAMMA + 1],
                                         bias=vec[:, V_BETA:V_BETA + 1]).then_inc(xnT_f32, 1)
                if ffn:
                    hidden_hi(f, 4)
                    gelu(f, 5, gnn)
                if gnn:
                    act.wait_ge(xc_pre, g + 1)
                    nc.scalar.activation(xc_h[:], xc[:], ACT.Relu).then_inc(xc_hi, 1)
                if ffn:
                    hidden_hi(f, 5)
                if gnn:
                    act.wait_ge(pe_nmp, g + 1)
                    nc.scalar.copy(nm_h, G0[:]).then_inc(nmp_hi, 1)
                if ffn:
                    gelu(f, 6, gnn)
                if tail:
                    act.wait_ge(rt_step, ROUTER_STEPS * d + ROUTER_GAP)
                    nc.scalar.activation(gap_t[:], gap[:], ACT.Tanh, scale=0.5).then_inc(gap_tanh, 1)
                if ffn:
                    hidden_hi(f, 6)
                if gnn:
                    act.wait_ge(pe_r, g + 1)
                    nc.scalar.activation(tr[:], G2[:], ACT.Tanh, scale=0.5,
                                         bias=dv[:, D_R:D_R + 1]).then_inc(r_tanh, 1)
                    act.wait_ge(pe_z, g + 1)
                    nc.scalar.activation(tz[:], G1[:], ACT.Tanh, scale=0.5,
                                         bias=dv[:, D_Z:D_Z + 1]).then_inc(z_tanh, 1)
                if ffn:
                    gelu(f, 7, gnn)
                    hidden_hi(f, 7)
                if tail:
                    act.wait_ge(pe_wT, d + 1)
                    nc.scalar.copy(wT, G2[0:EXPERTS, :]).then_inc(wT_f32, 1)
                    nc.scalar.copy(wT_s[:], G2[:]).then_inc(wT_hi, 1)
                if more:
                    act.wait_ge(pe_xT, g + 2)
                    act.wait_ge(xlT_kept, g + 1)
                    nc.scalar.copy(xlT[:], M[:]).then_inc(xlT_f32, 1)
                if gnn:
                    act.wait_ge(gate_step, 3 * g + 3)
                    nc.scalar.activation(nn[:], tr[:], ACT.Tanh, bias=vec[:, V_IH + 2:V_IH + 3]).then_inc(n_tanh, 1)
                if ffn:
                    act.wait_ge(pe_y, EXPERTS * f + EXPERTS)
                    nc.scalar.copy(y_s, Y[:]).then_inc(y_copied, 1)

            w_hi_part("first")
            act.wait_ge(pe_xT, 1)
            nc.scalar.copy(xlT[:], M[:]).then_inc(xlT_f32, 1)
            for name in ("conv_s", "conv_a"):
                w_hi_part(name)
            act.wait_ge(b2_loaded, 16)
            nc.scalar.copy(b2_s[:], b2_raw).then_inc(b2_hi, 1)
            for name in ("conv_b", "gates"):
                w_hi_part(name)
            act.wait_ge(vec_loaded, 16)
            act.wait_ge(dv_step, 5)
            run(act, iteration)

        @block.gpsimd
        def _(pool):
            def w_lo_part(name):
                first, blocks, raw = parts[name]
                cols = slice(first * P, (first + blocks) * P)
                pool.wait_ge(w_hi_done[name], 1)
                nc.gpsimd.tensor_tensor(w_lo[:, cols], raw, w_hi[:, cols].bitcast(F32),
                                        ALU.subtract).then_inc(w_lo_done[name], 1)

            def iteration(g, gnn, tail, ffn, more):
                d, f = g - 1, g - 2

                def hidden_lo(e):
                    for h in range(1 if is_graph(f, GRAPHS - 1) else HALVES):
                        n = 2 * e + h
                        slot = (e % RINGS) * HALVES + h
                        pool.wait_ge(hw_hi, 16 * f + n + 1)
                        nc.gpsimd.tensor_tensor(hw_l[:, slot, :], hw[:, n % SLOTS, :],
                                                hw_h[:, slot, :].bitcast(F32), ALU.subtract).then_inc(hw_lo, 1)

                if ffn:
                    hidden_lo(0)
                if tail:
                    pool.wait_ge(ln2_step, 3 * d + 3)
                    nc.gpsimd.tensor_tensor(rs[:], ve[:], cst[:, C_HALF:C_HALF + NT], ALU.pow).then_inc(ln2_rstd, 1)
                if ffn:
                    hidden_lo(1)
                if gnn:
                    if tail:
                        pool.wait_ge(gru_step, 3 * d + 3)
                    pool.wait_ge(both_f32, g + 1)
                    pairs = "p (m h) -> p m h"
                    nc.gpsimd.tensor_tensor(xc[:].rearrange(pairs, h=2), xlT[:].rearrange(pairs, h=2),
                                            both.unsqueeze(2).broadcast_to([P, HALF, 2]),
                                            ALU.add).then_inc(xc_base, 1)
                if ffn:
                    hidden_lo(2)
                if more:
                    pool.wait_ge(ln1_step, 3 * g + 6)
                    nc.gpsimd.tensor_tensor(rs[:], ve[:], cst[:, C_HALF:C_HALF + NT], ALU.pow).then_inc(ln1_rstd, 1)
                if ffn:
                    hidden_lo(3)
                if gnn:
                    for j in range(NT):
                        pool.wait_ge(a_hi, NT * g + j + 1)
                        nc.gpsimd.tensor_tensor(a_l[:, j, :], ex[:, j, :], a_h[:, j, :].bitcast(F32),
                                                ALU.subtract).then_inc(a_split, 1)
                if ffn:
                    hidden_lo(4)
                if is_graph(g, 0):
                    w_lo_part("w1")
                if is_graph(g, 1):
                    w_lo_part("w2")
                if ffn:
                    for e in (5, 6, 7):
                        hidden_lo(e)

            nc.gpsimd.memset(h1[:, 0:PAD], 0.0)
            nc.gpsimd.memset(h1[:, PAD + NODES:], 0.0).then_inc(zeroed, 1)
            nc.gpsimd.memset(w_tok[:], 0.0).then_inc(zeroed, 1)
            pool.wait_ge(cst_loaded, 16)
            pool.wait_ge(dv_step, 1)
            nc.gpsimd.tensor_tensor(dv[:, 6:8], dv[:, 6:8], cst[:, C_HALF:C_HALF + 2], ALU.pow).then_inc(dv_pow, 1)
            pool.wait_ge(ln1_step, 3)
            nc.gpsimd.tensor_tensor(rs[:], ve[:], cst[:, C_HALF:C_HALF + NT], ALU.pow).then_inc(ln1_rstd, 1)
            pool.wait_ge(w_loaded["conv_a"], 16)
            pool.wait_ge(w_loaded["conv_b"], 16)
            nc.gpsimd.tensor_tensor(parts["conv_s"][2], parts["conv_a"][2][:, 0:TAPS_B * P], parts["conv_b"][2],
                                    ALU.add).then_inc(conv_summed, 1)
            w_lo_part("conv_b")
            w_lo_part("gates")
            run(pool, iteration)

        @block.vector
        def _(dve):
            def w_lo_part(name):
                first, blocks, raw = parts[name]
                cols = slice(first * P, (first + blocks) * P)
                dve.wait_ge(w_hi_done[name], 1)
                nc.vector.tensor_tensor(w_lo[:, cols], raw, w_hi[:, cols].bitcast(F32),
                                        ALU.subtract).then_inc(w_lo_done[name], 1)

            def v2(tile):
                return tile[:, :, :].rearrange("p t d -> p (t d)")

            def split(src, dst_h, dst_l, hi_done, lo_done, g):
                nc.vector.tensor_copy(dst_h, src).then_inc(hi_done, 1)
                dve.wait_ge(hi_done, g + 1)
                nc.vector.tensor_tensor(dst_l, src, dst_h.bitcast(F32), ALU.subtract).then_inc(lo_done, 1)

            def stack(tile, src, pattern, a=0, b=P):
                return nc.vector.scalar_tensor_tensor(out=tile[a:b, :], in0=tile[a:b, :].bitcast(F32),
                                                      scalar=cst[a:b, pattern:pattern + 1], in1=src[a:b, :],
                                                      op0=ALU.mult, op1=ALU.add)

            def carry_wait():
                nc.vector.memset(spare[:], 0.0)

            def statistics(src, step, g, scale, bias):
                for t in range(NT):
                    last = nc.vector.bn_stats(st[:, t, :], src[:, t, :])
                last.then_inc(step, 1)
                dve.wait_ge(step, 3 * g + 1)
                carry_wait()
                for t in range(NT):
                    last = nc.vector.bn_aggr(mv[:, t, :], st[:, t, :])
                last.then_inc(step, 1)
                dve.wait_ge(step, 3 * g + 2)
                nc.vector.tensor_scalar(ve[:], mv[:, :, 1], scale, bias, ALU.mult, ALU.add).then_inc(step, 1)

            def normalize(dst, src, rstd_done, ready, g):
                dve.wait_ge(rstd_done, g + 1)
                for t in range(NT):
                    last = nc.vector.tensor_scalar(dst[:, t, :], src[:, t, :], mv[:, t, 0:1], rs[:, t:t + 1],
                                                   ALU.subtract, ALU.mult)
                last.then_inc(ready, 1)

            def router_steps(d):
                done = [0]

                def step(instruction):
                    done[0] += 1
                    instruction.then_inc(rt_step, 1)
                    dve.wait_ge(rt_step, ROUTER_STEPS * d + done[0])

                def choose():
                    dve.wait_ge(pe_router, d + 1)
                    bias = vec[:, V_BR:V_BR + EXPERTS].unsqueeze(1).broadcast_to([P, NT, EXPERTS])
                    step(nc.vector.tensor_tensor(lg[:], M[:, 0:NT * EXPERTS].rearrange("p (t e) -> p t e", t=NT), bias,
                                                 ALU.add))
                    carry_wait()
                    for t in range(NT):
                        last = nc.vector.max(top[:, t, :], lg[:, t, :])
                    step(last)
                    nc.vector.tensor_tensor(gap[:], top[:, :, 0], top[:, :, 1], ALU.subtract).then_inc(rt_step, 1)
                    done[0] += 1
                    assert done[0] == ROUTER_GAP
                    for t in range(NT):
                        last = nc.vector.max_index(top_i[:, t, :], top[:, t, :], lg[:, t, :])
                    step(last)
                    step(nc.vector.tensor_copy(pick[:], top_i[:, :, 0:2]))

                def weights_of():
                    iota = cst[:, C_IOTA:C_IOTA + EXPERTS].unsqueeze(1).broadcast_to([P, NT * 2, EXPERTS])
                    hots = hot[:, :, :, :].rearrange("p t k e -> p (t k) e")
                    picks = pick[:, :, :].rearrange("p t k -> p (t k)").unsqueeze(2)
                    nc.vector.tensor_tensor(hots, iota, picks.broadcast_to([P, NT * 2, EXPERTS]), ALU.is_equal)
                    dve.wait_ge(gap_tanh, d + 1)
                    nc.vector.tensor_scalar(w12[:, :, 0], gap_t[:], 0.5, 0.5, ALU.mult, ALU.add)
                    step(nc.vector.tensor_scalar(w12[:, :, 1], gap_t[:], -0.5, 0.5, ALU.mult, ALU.add))
                    w12s = w12[:, :, :].rearrange("p t k -> p (t k)").unsqueeze(2)
                    step(nc.vector.tensor_tensor(hots, hots, w12s.broadcast_to([P, NT * 2, EXPERTS]), ALU.mult))
                    for r in range(4):
                        last = nc.vector.tensor_tensor(w_tok[:, :, 32 * r:32 * r + EXPERTS], hot[:, :, 0, :],
                                                       hot[:, :, 1, :], ALU.add)
                    step(last)
                    assert done[0] == ROUTER_STEPS

                return choose, weights_of

            def operands_lo(g):
                dve.wait_ge(uv_hi, g + 1)
                stack(u_s, s_f, C_DU, 0, 96)
                stack(v_s, s_f, C_DV, 0, 64)
                stack(v_s, s_f, C_DV, 96, P).then_inc(uv_split, 1)

            def gru(g):
                dve.wait_ge(n_tanh, g + 1)
                nc.vector.tensor_tensor(gr[:], xlT_keep[:], nn[:], ALU.subtract).then_inc(gru_step, 1)
                dve.wait_ge(z_tanh, g + 1)
                dve.wait_ge(gru_step, 3 * g + 1)
                nc.vector.scalar_tensor_tensor(out=gr[:], in0=tz[:], scalar=1.0, in1=gr[:], op0=ALU.add,
                                               op1=ALU.mult).then_inc(gru_step, 1)
                dve.wait_ge(gru_step, 3 * g + 2)
                nc.vector.scalar_tensor_tensor(out=gr[:], in0=gr[:], scalar=0.5, in1=nn[:], op0=ALU.mult,
                                               op1=ALU.add).then_inc(gru_step, 1)

            def weigh(f, e):
                for h in range(HALVES):
                    n = 2 * e + h
                    dve.wait_ge(gelu_done, 16 * f + n + 1)
                    if h == 0:
                        dve.wait_ge(wb_loaded[e % 2], 64 * f + 16 * (e // 2) + 16)
                    if n >= SLOTS:
                        wait_split(dve, f, n - SLOTS)
                    nc.vector.tensor_tensor(hw[:, n % SLOTS, :], ge[:, n % SLOTS, :], wb[:, e % 2, :],
                                            ALU.mult).then_inc(hw_f32, 1)
                if is_graph(f, GRAPHS - 1):
                    n = 2 * e + 1
                    slot = (e % RINGS) * HALVES + 1
                    dve.wait_ge(hw_hi, 16 * f + n + 1)
                    nc.vector.tensor_tensor(hw_l[:, slot, :], hw[:, n % SLOTS, :], hw_h[:, slot, :].bitcast(F32),
                                            ALU.subtract).then_inc(hw_lo_dve, 1)

            def iteration(g, gnn, tail, ffn, more):
                d, f = g - 1, g - 2

                def differences():
                    if tail and ffn:
                        dve.wait_ge(w_stored, 16 * f + 16)
                    nc.vector.tensor_tensor(diff[:, 0, :], h1[:, 0:PADDED:2], h1[:, 1:PADDED:2], ALU.subtract)
                    nc.vector.tensor_tensor(diff[:, 1, :], h1[:, 2:PADDED + 2:2], h1[:, 1:PADDED:2],
                                            ALU.subtract).then_inc(diff_f32, 1)
                    dve.wait_ge(diff_f32, g + 1)
                    split(diff[:], cv_h[:, 0:2, :], cv_l[:, 0:2, :], diff_hi, diff_split, g)

                if tail:
                    choose, weights_of = router_steps(d)
                if gnn:
                    dve.wait_ge(h1_f32, g + 1)
                    split(h1[:, 1:PADDED:2], cv_h[:, 2, :], cv_l[:, 2, :], odd_hi, odd_split, g)
                    if is_graph(g, 1):
                        gru(d)
                    if not ffn:
                        differences()
                        operands_lo(g)
                if ffn:
                    weigh(f, 0)
                    weigh(f, 1)
                if tail:
                    if ffn:
                        if not is_graph(f, 0):
                            dve.wait_ge(final_done, f)
                        nc.vector.tensor_copy(x1_keep[:], x1[:]).then_inc(x1_kept, 1)
                    dve.wait_ge(pe_outT, d + 1)
                    dve.wait_ge(x_res_loaded, 16 * d + 16)
                    if ffn:
                        dve.wait_ge(x1_kept, f + 1)
                    nc.vector.tensor_tensor(v2(x1), v2(x_res), G2[:], ALU.add).then_inc(x1_ready, 1)
                    dve.wait_ge(x1_ready, d + 1)
                    statistics(x1, ln2_step, d, 1.0 + EPS, EPS * EPS)
                if ffn:
                    if gnn:
                        differences()
                    weigh(f, 2)
                if gnn:
                    if ffn:
                        operands_lo(g)
                    dve.wait_ge(msg_hi, g + 1)
                    nc.vector.tensor_tensor(v2(msg_l), M[:], v2(msg_h).bitcast(F32),
                                            ALU.subtract).then_inc(msg_split, 1)
                if tail:
                    if ffn and not is_graph(f, 0):
                        dve.wait_ge(out_stored, 16 * f)
                    normalize(xn, x1, ln2_rstd, xn_ready, d)
                if ffn:
                    weigh(f, 3)
                if more:
                    dve.wait_ge(x_ln_loaded, 16 * g + 32)
                    statistics(x_ln, ln1_step, g + 1, 1.0, EPS)
                if gnn:
                    dve.wait_ge(adj_loaded, 16 * g + 16)
                    for j in range(NT):
                        dve.wait_ge(exp_done, NT * g + j + 1)
                        nc.vector.tensor_tensor(ex[:, j, :], ex[:, j, :], adj[:, j, :], ALU.mult).then_inc(a_prod, 1)
                        dve.wait_ge(a_prod, NT * g + j + 1)
                        nc.vector.tensor_copy(a_h[:, j, :], ex[:, j, :]).then_inc(a_hi, 1)
                        if j == 1 and more:
                            normalize(xl, x_ln, ln1_rstd, xl_ready, g + 1)
                    nc.vector.tensor_copy(xlT_keep[:], xlT[:]).then_inc(xlT_kept, 1)
                if ffn:
                    weigh(f, 4)
                if gnn:
                    dve.wait_ge(pe_conv2, g + 1)
                    dve.wait_ge(xc_base, g + 1)
                    pairs = xc[:].rearrange("p (m h) -> p m h", h=2)
                    nc.vector.scalar_tensor_tensor(out=pairs, in0=C2[:].rearrange("p (h m) -> p m h", h=2),
                                                   scalar=dv[:, D_SC2:D_SC2 + 1], in1=pairs, op0=ALU.mult,
                                                   op1=ALU.add).then_inc(xc_pre, 1)
                if ffn:
                    weigh(f, 5)
                if gnn:
                    dve.wait_ge(xc_hi, g + 1)
                    nc.vector.scalar_tensor_tensor(out=xc_l[:], in0=xc[:], scalar=0.0, in1=xc_h[:].bitcast(F32),
                                                   op0=ALU.max, op1=ALU.subtract).then_inc(xc_split, 1)
                if tail:
                    choose()
                if gnn:
                    dve.wait_ge(nmp_hi, g + 1)
                    nc.vector.tensor_tensor(nm_l, G0[:], nm_h.bitcast(F32), ALU.subtract).then_inc(nmp_split, 1)
                if ffn:
                    weigh(f, 6)
                if tail:
                    weights_of()
                if gnn:
                    dve.wait_ge(r_tanh, g + 1)
                    nc.vector.tensor_scalar(tr[:], tr[:], 0.5, 0.5, ALU.mult, ALU.add).then_inc(gate_step, 1)
                if ffn:
                    weigh(f, 7)
                if tail:
                    if ffn:
                        dve.wait_ge(pe_h, 16 * f + 16)
                    split(xnT[:], xnT_h[:], xnT_l[:], xnT_hi, xnT_split, d)
                if tail:
                    dve.wait_ge(wT_hi, d + 1)
                    stack(wT_s, G2, C_GV).then_inc(wT_split, 1)
                if more:
                    dve.wait_ge(xlT_f32, g + 2)
                    split(xlT[:], xlT_h[:], xlT_l[:], xlT_hi, xlT_split, g + 1)
                if gnn:
                    dve.wait_ge(pe_n, g + 1)
                    dve.wait_ge(gate_step, 3 * g + 1)
                    nc.vector.scalar_tensor_tensor(out=tr[:], in0=G0[:], scalar=vec[:, V_HH + 2:V_HH + 3], in1=tr[:],
                                                   op0=ALU.add, op1=ALU.mult).then_inc(gate_step, 1)
                    dve.wait_ge(gate_step, 3 * g + 2)
                    nc.vector.tensor_tensor(tr[:], tr[:], C2[:], ALU.add).then_inc(gate_step, 1)
                if gnn and not is_graph(g, 0):
                    gru(g)
                if ffn:
                    dve.wait_ge(pe_yT, f + 1)
                    kept = x1_keep if tail else x1
                    if not tail:
                        dve.wait_ge(out_stored, 16 * f)
                    nc.vector.tensor_tensor(v2(o_s), v2(kept), Y[:], ALU.add).then_inc(final_done, 1)

            nc.vector.memset(u_s[96:P, :].bitcast(F32), -0.5)
            nc.vector.memset(v_s[64:96, :].bitcast(F32), -0.5).then_inc(rows_set, 1)
            dve.wait_ge(vec_loaded, 16)
            nc.vector.tensor_scalar(dv[:, 6:8], vec[:, V_V1:V_V2 + 1], EPS, None, ALU.add).then_inc(dv_step, 1)
            nc.vector.tensor_tensor(dv[:, D_R:D_Z + 1], vec[:, V_IH:V_IH + 2], vec[:, V_HH:V_HH + 2],
                                    ALU.add).then_inc(dv_step, 1)
            dve.wait_ge(dv_step, 2)
            nc.vector.tensor_scalar(dv[:, D_R:D_Z + 1], dv[:, D_R:D_Z + 1], 0.5, None, ALU.mult)
            dve.wait_ge(dv_pow, 1)
            nc.vector.tensor_tensor(dv[:, D_SC1:D_SC2 + 1], vec[:, V_G1:V_G2 + 1], dv[:, 6:8],
                                    ALU.mult).then_inc(dv_step, 1)
            dve.wait_ge(dv_step, 3)
            nc.vector.tensor_tensor(dv[:, D_BI1:D_BI2 + 1], vec[:, V_M1:V_M2 + 1], dv[:, D_SC1:D_SC2 + 1],
                                    ALU.mult).then_inc(dv_step, 1)
            dve.wait_ge(dv_step, 4)
            nc.vector.tensor_tensor(dv[:, D_BI1:D_BI2 + 1], vec[:, V_B1:V_B2 + 1], dv[:, D_BI1:D_BI2 + 1],
                                    ALU.subtract).then_inc(dv_step, 1)
            dve.wait_ge(cst_loaded, 16)
            dve.wait_ge(x_ln_loaded, 16)
            statistics(x_ln, ln1_step, 0, 1.0, EPS)
            normalize(xl, x_ln, ln1_rstd, xl_ready, 0)
            w_lo_part("first")
            dve.wait_ge(xlT_f32, 1)
            split(xlT[:], xlT_h[:], xlT_l[:], xlT_hi, xlT_split, 0)
            w_lo_part("conv_s")
            w_lo_part("conv_a")
            dve.wait_ge(b2_hi, 1)
            stack(b2_s, b2_raw, C_GU).then_inc(stacked, 1)
            dve.wait_ge(zeroed, 1)
            run(dve, iteration)


ROUTER_GAP = 3
ROUTER_STEPS = 8


def kernel(**inputs):
    import concourse.bacc as bacc
    from concourse.bass_utils import run_bass_kernel_spmd

    a = {k: np.asarray(v) for k, v in inputs.items()}
    g = {k.removeprefix("L0_gnn_"): v for k, v in a.items()}
    e = {k.removeprefix("L0_ffn_"): v for k, v in a.items()}

    w = np.zeros((P, WCOLS), np.float32)
    b2 = np.zeros((P, P), np.float32)

    def put(block, value):
        w[:value.shape[0], block * P:block * P + value.shape[1]] = value

    for r in range(4):
        b2[32 * r:32 * r + EXPERTS] = e["b2"]
    for row in S_ROWS:
        w[:, SE * P + row:SE * P + row + SPACE] = g["w_se"].T
    put(CONV1, g["conv1_w"][:, :, 0].T)
    put(MSG, g["w_msg"].T)
    for tap in range(TAPS):
        put((CONV_B if tap % 2 else CONV_A) + tap // 2, g["conv2_w"][:, :, tap].T)
    for gate in range(3):
        rows = slice(gate * P, (gate + 1) * P)
        put(IH + gate, g["w_ih"][rows, 0:P].T)
        put(IH + 3 + gate, g["w_ih"][rows, P:2 * P].T)
        put(HH + gate, g["w_hh"][rows].T)
    for n in range(EXPERTS):
        for h in range(HALVES):
            half = slice(h * P, (h + 1) * P)
            put(W1 + 2 * n + h, e["W1"][n][:, half])
            put(W2 + 2 * n + h, e["W2"][n][half, :])

    v = np.zeros((P, VCOLS), np.float32)
    for col, name in ((V_G1, "bn1_g"), (V_G2, "bn2_g"), (V_V1, "bn1_v"), (V_V2, "bn2_v"), (V_B1, "bn1_b"),
                      (V_B2, "bn2_b"), (V_M1, "bn1_m"), (V_M2, "bn2_m")):
        v[:, col] = g[name]
    for gate in range(3):
        v[:, V_IH + gate] = g["b_ih"][gate * P:(gate + 1) * P]
        v[:, V_HH + gate] = g["b_hh"][gate * P:(gate + 1) * P]
    v[:, V_GAMMA] = e["gamma"]
    v[:, V_BETA] = e["beta"]
    for row in S_ROWS:
        v[row:row + SPACE, V_SE] = g["b_se"]
    for n in range(EXPERTS):
        for h in range(HALVES):
            v[:, V_EB1 + 2 * n + h] = e["b1"][n, h * P:(h + 1) * P]
    v[:, V_BR:V_BR + EXPERTS] = e["br"]
    v[:, V_BM] = g["b_msg"]
    v[:, V_WR:V_WR + EXPERTS] = e["Wr"]

    arrays = {
        "x": np.ascontiguousarray(a["x"]),
        "adj_t": np.ascontiguousarray(a["adj"].transpose(0, 2, 1)),
        "weights": w,
        "b2_rows": b2,
        "vectors": v,
        "consts": constants(),
    }
    nc = bacc.Bacc("TRN2", target_bir_lowering=False, num_devices=1)
    args = [nc.dram_tensor(n, t.shape, F32, kind="ExternalInput").ap() for n, t in arrays.items()]
    w_rows = nc.dram_tensor("w_rows", (EXPERTS, NODES), F32, kind="Internal").ap()
    out = nc.dram_tensor("out", a["x"].shape, F32, kind="ExternalOutput").ap()
    gnn_moe(nc, *args, w_rows, out)
    result = run_bass_kernel_spmd(nc, [arrays], core_ids=[0])
    return result.results[0]["out"]
```
